# Optimizing a Trainium2 kernel written in Bass

```python
import numpy as np
import jax
import jax.numpy as jnp

def _softmax(x, axis=-1):
    return jax.nn.softmax(x, axis=axis)

def _gelu(x):
    return jax.nn.gelu(x, approximate=True)

def _silu(x):
    return jax.nn.silu(x)

def _sigmoid(x):
    return jax.nn.sigmoid(x)

def _layernorm(x, axis=-1, eps=1e-05):
    m = jnp.mean(x, axis=axis, keepdims=True)
    v = jnp.var(x, axis=axis, keepdims=True)
    return (x - m) / jnp.sqrt(v + eps)

def _scatter_add(tgt, idx, src, axis=0):
    return tgt.at[idx].add(src)

def _segment_sum(src, seg, n):
    return jax.ops.segment_sum(src, seg, n)
kernel_name = 'mk_audio_tower_d1_tok_audfeat512_r4_9c254a'

def setup_inputs(seed: int=0):
    np.random.seed(seed)
    _w = jnp.asarray

    def _rec_inputs():
        import jax
        import jax.numpy as jnp
        _rk = jax.random.key(seed)
        x = 7.22013e-05 + 1.00017 * jax.random.normal(jax.random.fold_in(_rk, 1), (16, 750, 64), jnp.float32)
        return x
    x = _rec_inputs()

    def _L0_tok_setup():
        import jax, jax.numpy as jnp
        import numpy as np
        EPS = 1e-07
        C_CURV = 1.0
        LAM_HALF = 1.0 / (1.0 + EPS)
        key = jax.random.key(seed)
        k1, k2 = jax.random.split(key)
        B, L, Cin, K, F = (32, 256, 64, 9, 128)
        x = jax.random.normal(k1, (B, L, Cin), dtype=jnp.float32)
        lim = float(np.sqrt(6.0 / (K * Cin + F)))
        kernel = jax.random.uniform(k2, (K, Cin, F), dtype=jnp.float32, minval=-lim, maxval=lim)
        bias = jnp.zeros((F,), dtype=jnp.float32)
        return {'x': x, 'kernel': kernel, 'bias': bias}
    _L0_tok_all = _L0_tok_setup()
    _L0_tok_in = {k: v for k, v in _L0_tok_all.items() if k in ('kernel', 'bias')}
    del _L0_tok_all

    def _L0_attn_setup():
        import jax, jax.numpy as jnp
        import numpy as np
        EPS_L2 = 1e-12
        EPS_NORM = 1e-05

        def _linear(x, W, b):
            return x @ W.T + b

        def _silu(x):
            return x * jax.nn.sigmoid(x)

        def _l2norm(x):
            n = jnp.sqrt(jnp.sum(x * x, axis=-1, keepdims=True))
            return x / jnp.maximum(n, EPS_L2)

        def _dwconv_causal(x, w, b):
            y = jax.lax.conv_general_dilated(x.transpose(0, 2, 1), w, window_strides=(1,), padding=[(3, 0)], dimension_numbers=('NCH', 'OIH', 'NCH'), feature_group_count=w.shape[0])
            return y.transpose(0, 2, 1) + b

        def _zc_rmsnorm(x, weight):
            xm = x - jnp.mean(x, axis=-1, keepdims=True)
            var = jnp.mean(xm * xm, axis=-1, keepdims=True)
            return xm * jax.lax.rsqrt(var + EPS_NORM) * weight

        def _gated_delta_core(q, k, v, alpha, beta):
            B, S, d = q.shape
            S0 = jnp.zeros((B, d, d), dtype=q.dtype)

            def step(St, inp):
                qt, kt, vt, at, bt = inp
                Sk = jnp.einsum('bij,bj->bi', St, kt)
                a = at[:, None, None]
                b = bt[:, None, None]
                Sn = a * (St - b * Sk[:, :, None] * kt[:, None, :]) + b * vt[:, :, None] * kt[:, None, :]
                ot = jnp.einsum('bij,bj->bi', Sn, qt)
                return (Sn, ot)
            xs = (q.transpose(1, 0, 2), k.transpose(1, 0, 2), v.transpose(1, 0, 2), alpha.T, beta.T)
            _, outs = jax.lax.scan(step, S0, xs)
            return outs.transpose(1, 0, 2)
        key = jax.random.key(seed)
        ks = jax.random.split(key, 16)
        B, S, d = (8, 512, 128)
        w = lambda k, shape: jax.random.normal(k, shape, jnp.float32) * 0.02
        return {'x': jax.random.normal(ks[0], (B, S, d), jnp.float32), 'Wq': w(ks[1], (d, d)), 'bq': jnp.zeros((d,), jnp.float32), 'Wk': w(ks[2], (d, d)), 'bk': jnp.zeros((d,), jnp.float32), 'Wv': w(ks[3], (d, d)), 'bv': jnp.zeros((d,), jnp.float32), 'Wa': w(ks[4], (1, d)), 'ba': jnp.zeros((1,), jnp.float32), 'Wb': w(ks[5], (1, d)), 'bb': jnp.zeros((1,), jnp.float32), 'cwq': w(ks[6], (d, 1, 4)), 'cbq': jnp.zeros((d,), jnp.float32), 'cwk': w(ks[7], (d, 1, 4)), 'cbk': jnp.zeros((d,), jnp.float32), 'cwv': w(ks[8], (d, 1, 4)), 'cbv': jnp.zeros((d,), jnp.float32), 'norm_w': jnp.ones((d,), jnp.float32), 'Wg': w(ks[9], (d, d)), 'bg': jnp.zeros((d,), jnp.float32), 'Wo': w(ks[10], (d, d)), 'bo': jnp.zeros((d,), jnp.float32)}
    _L0_attn_all = _L0_attn_setup()
    _L0_attn_in = {k: v for k, v in _L0_attn_all.items() if k in ('Wq', 'bq', 'Wk', 'bk', 'Wv', 'bv', 'Wa', 'ba', 'Wb', 'bb', 'cwq', 'cbq', 'cwk', 'cbk', 'cwv', 'cbv', 'norm_w', 'Wg', 'bg', 'Wo', 'bo')}
    del _L0_attn_all

    def _L0_ffn_setup():
        import jax, jax.numpy as jnp
        import numpy as np
        B, T, D = (4, 2048, 128)
        E, F, CAP = (8, 512, 1024)
        key = jax.random.key(seed)
        ks = jax.random.split(key, 6)
        s = 0.02
        return {'x': jax.random.normal(ks[0], (B, T, D), dtype=jnp.float32), 'Wr': jax.random.normal(ks[1], (D, E), dtype=jnp.float32) * s, 'W1': jax.random.normal(ks[2], (E, D, F), dtype=jnp.float32) * s, 'b1': jax.random.normal(ks[3], (E, F), dtype=jnp.float32) * s, 'W2': jax.random.normal(ks[4], (E, F, D), dtype=jnp.float32) * s, 'b2': jax.random.normal(ks[5], (E, D), dtype=jnp.float32) * s}
    _L0_ffn_all = _L0_ffn_setup()
    _L0_ffn_in = {k: v for k, v in _L0_ffn_all.items() if k in ('Wr', 'W1', 'b1', 'W2', 'b2')}
    del _L0_ffn_all
    return {'x': x, 'L0_tok_kernel': _L0_tok_in['kernel'], 'L0_tok_bias': _L0_tok_in['bias'], 'L0_attn_Wq': _L0_attn_in['Wq'], 'L0_attn_bq': _L0_attn_in['bq'], 'L0_attn_Wk': _L0_attn_in['Wk'], 'L0_attn_bk': _L0_attn_in['bk'], 'L0_attn_Wv': _L0_attn_in['Wv'], 'L0_attn_bv': _L0_attn_in['bv'], 'L0_attn_Wa': _L0_attn_in['Wa'], 'L0_attn_ba': _L0_attn_in['ba'], 'L0_attn_Wb': _L0_attn_in['Wb'], 'L0_attn_bb': _L0_attn_in['bb'], 'L0_attn_cwq': _L0_attn_in['cwq'], 'L0_attn_cbq': _L0_attn_in['cbq'], 'L0_attn_cwk': _L0_attn_in['cwk'], 'L0_attn_cbk': _L0_attn_in['cbk'], 'L0_attn_cwv': _L0_attn_in['cwv'], 'L0_attn_cbv': _L0_attn_in['cbv'], 'L0_attn_norm_w': _L0_attn_in['norm_w'], 'L0_attn_Wg': _L0_attn_in['Wg'], 'L0_attn_bg': _L0_attn_in['bg'], 'L0_attn_Wo': _L0_attn_in['Wo'], 'L0_attn_bo': _L0_attn_in['bo'], 'L0_ffn_Wr': _L0_ffn_in['Wr'], 'L0_ffn_W1': _L0_ffn_in['W1'], 'L0_ffn_b1': _L0_ffn_in['b1'], 'L0_ffn_W2': _L0_ffn_in['W2'], 'L0_ffn_b2': _L0_ffn_in['b2']}

def reference(x, L0_tok_kernel, L0_tok_bias, L0_attn_Wq, L0_attn_bq, L0_attn_Wk, L0_attn_bk, L0_attn_Wv, L0_attn_bv, L0_attn_Wa, L0_attn_ba, L0_attn_Wb, L0_attn_bb, L0_attn_cwq, L0_attn_cbq, L0_attn_cwk, L0_attn_cbk, L0_attn_cwv, L0_attn_cbv, L0_attn_norm_w, L0_attn_Wg, L0_attn_bg, L0_attn_Wo, L0_attn_bo, L0_ffn_Wr, L0_ffn_W1, L0_ffn_b1, L0_ffn_W2, L0_ffn_b2):
    import jax
    import jax.numpy as jnp

    def _L0_tok_ref(x, kernel, bias):
        import jax, jax.numpy as jnp
        import numpy as np
        EPS = 1e-07
        C_CURV = 1.0
        LAM_HALF = 1.0 / (1.0 + EPS)
        B, L, Cin = x.shape
        K, _, F = kernel.shape
        Lout = L - K + 1
        sq = jnp.sum(x * x, axis=-1)
        cs = jnp.concatenate([jnp.zeros((B, 1), x.dtype), jnp.cumsum(sq, axis=1)], axis=1)
        wsq = cs[:, K:] - cs[:, :Lout]
        wnorm = jnp.sqrt(jnp.maximum(wsq, 0.0))
        scale = jnp.where(wnorm < 1.0, 1.0, 1.0 / (wnorm + EPS))[..., None]
        conv = jax.lax.conv_general_dilated(x, kernel, window_strides=(1,), padding='VALID', dimension_numbers=('NWC', 'WIO', 'NWC'))
        v = conv * scale
        v_norm = jnp.maximum(jnp.abs(v), EPS)
        y = jnp.tanh(v_norm * LAM_HALF) * (v / v_norm)
        return jax.nn.relu(y + bias)

    def _L0_attn_ref(x, Wq, bq, Wk, bk, Wv, bv, Wa, ba, Wb, bb, cwq, cbq, cwk, cbk, cwv, cbv, norm_w, Wg, bg, Wo, bo):
        import jax, jax.numpy as jnp
        import numpy as np
        EPS_L2 = 1e-12
        EPS_NORM = 1e-05

        def _linear(x, W, b):
            return x @ W.T + b

        def _silu(x):
            return x * jax.nn.sigmoid(x)

        def _l2norm(x):
            n = jnp.sqrt(jnp.sum(x * x, axis=-1, keepdims=True))
            return x / jnp.maximum(n, EPS_L2)

        def _dwconv_causal(x, w, b):
            y = jax.lax.conv_general_dilated(x.transpose(0, 2, 1), w, window_strides=(1,), padding=[(3, 0)], dimension_numbers=('NCH', 'OIH', 'NCH'), feature_group_count=w.shape[0])
            return y.transpose(0, 2, 1) + b

        def _zc_rmsnorm(x, weight):
            xm = x - jnp.mean(x, axis=-1, keepdims=True)
            var = jnp.mean(xm * xm, axis=-1, keepdims=True)
            return xm * jax.lax.rsqrt(var + EPS_NORM) * weight

        def _gated_delta_core(q, k, v, alpha, beta):
            B, S, d = q.shape
            S0 = jnp.zeros((B, d, d), dtype=q.dtype)

            def step(St, inp):
                qt, kt, vt, at, bt = inp
                Sk = jnp.einsum('bij,bj->bi', St, kt)
                a = at[:, None, None]
                b = bt[:, None, None]
                Sn = a * (St - b * Sk[:, :, None] * kt[:, None, :]) + b * vt[:, :, None] * kt[:, None, :]
                ot = jnp.einsum('bij,bj->bi', Sn, qt)
                return (Sn, ot)
            xs = (q.transpose(1, 0, 2), k.transpose(1, 0, 2), v.transpose(1, 0, 2), alpha.T, beta.T)
            _, outs = jax.lax.scan(step, S0, xs)
            return outs.transpose(1, 0, 2)
        q_c = _dwconv_causal(_linear(x, Wq, bq), cwq, cbq)
        k_c = _dwconv_causal(_linear(x, Wk, bk), cwk, cbk)
        v_c = _dwconv_causal(_linear(x, Wv, bv), cwv, cbv)
        q = _l2norm(_silu(q_c))
        k = _l2norm(_silu(k_c))
        v = _silu(v_c)
        alpha = jax.nn.sigmoid(_linear(x, Wa, ba))[..., 0]
        beta = jax.nn.sigmoid(_linear(x, Wb, bb))[..., 0]
        gdn = _gated_delta_core(q, k, v, alpha, beta)
        gdn = _zc_rmsnorm(gdn, norm_w)
        gate = _silu(_linear(x, Wg, bg))
        return _linear(gdn * gate, Wo, bo)

    def _L0_ffn_ref(x, Wr, W1, b1, W2, b2):
        import jax, jax.numpy as jnp
        import numpy as np
        B, T, D = (4, 2048, 128)
        E, F, CAP = (8, 512, 1024)
        Bb, Tt, Dd = x.shape
        N = Bb * Tt
        C = min(CAP, N)
        x_flat = x.reshape(N, Dd)
        logits = x_flat @ Wr
        probs = jax.nn.softmax(logits, axis=0)
        vals, idx = jax.lax.top_k(probs.T, C)
        selected = x_flat[idx]
        h = jax.nn.gelu(jnp.einsum('ecd,edf->ecf', selected, W1) + b1[:, None, :], approximate=False)
        out_e = jnp.einsum('ecf,efd->ecd', h, W2) + b2[:, None, :]
        weighted = vals[..., None] * out_e
        output = jnp.zeros_like(x_flat).at[idx.reshape(-1)].add(weighted.reshape(-1, Dd))
        return output.reshape(Bb, Tt, Dd)
    h = _L0_tok_ref(x, L0_tok_kernel, L0_tok_bias)
    h = h + _L0_attn_ref(_layernorm(h, axis=-1), L0_attn_Wq, L0_attn_bq, L0_attn_Wk, L0_attn_bk, L0_attn_Wv, L0_attn_bv, L0_attn_Wa, L0_attn_ba, L0_attn_Wb, L0_attn_bb, L0_attn_cwq, L0_attn_cbq, L0_attn_cwk, L0_attn_cbk, L0_attn_cwv, L0_attn_cbv, L0_attn_norm_w, L0_attn_Wg, L0_attn_bg, L0_attn_Wo, L0_attn_bo)
    h = h + _L0_ffn_ref(_layernorm(h, axis=-1), L0_ffn_Wr, L0_ffn_W1, L0_ffn_b1, L0_ffn_W2, L0_ffn_b2)
    return h

_drawn_inputs = setup_inputs


def setup_inputs(seed=0):
    import zlib

    import numpy as np

    out = dict(_drawn_inputs(seed))
    spreads = {'L0_tok_bias': (0.0, 0.1),
     'L0_attn_bq': (0.0, 0.8),
     'L0_attn_bk': (0.0, 2.0),
     'L0_attn_bv': (0.0, 0.8),
     'L0_attn_cbq': (0.0, 0.615),
     'L0_attn_cbk': (0.0, 0.613),
     'L0_attn_cbv': (0.0, 0.1),
     'L0_attn_norm_w': (1.0, 0.6),
     'L0_attn_bg': (0.0, 0.1),
     'L0_attn_bo': (0.0, 0.1)}
    factors = {'L0_attn_Wq': 8.0,
     'L0_attn_Wk': 8.0,
     'L0_attn_Wv': 3.314,
     'L0_attn_Wa': 30.628,
     'L0_attn_Wb': 8.0,
     'L0_attn_cwq': 8.0,
     'L0_attn_cwk': 8.0,
     'L0_attn_cwv': 3.738,
     'L0_ffn_Wr': 64.0,
     'L0_ffn_W1': 64.0,
     'L0_ffn_b1': 64.0,
     'L0_ffn_W2': 64.0,
     'L0_ffn_b2': 64.0}
    for name, (base, spread) in spreads.items():
        noise = np.random.default_rng([zlib.crc32(name.encode()), seed]).standard_normal(out[name].shape)
        drawn = base * np.exp(spread * noise) if base else spread * noise
        out[name] = jnp.asarray(drawn.astype(out[name].dtype))
    for name, factor in factors.items():
        out[name] = (out[name] * factor).astype(out[name].dtype)
    return out
```

```python
from contextlib import ExitStack

import numpy as np
import concourse.bass as bass
from concourse import mybir
from concourse.alu_op_type import AluOpType as ALU

B, LX, CIN = 16, 750, 64
TAPS, F = 9, 128
L = LX - TAPS + 1
T = 106
CH = L // T
XR = T + TAPS - 2
XS = XR + 1
Q = 4
W = Q * T
OCT = B // (2 * Q)
E, FF, CAP = 8, 512, 1024
N = B * L
ST = CAP // 128
DW = 4
HALO = DW - 1
LEVELS = 7
TILES = N // T
HI, LO = 64, 16
assert CH * T == L and HI * LO == CAP and B * E == 128

IDENT, TRI_LE, TRI_GT, BAND = 0, 128, 128 + T, 128 + 2 * T
CENTRE = BAND + T
MEAN, ONES, GROUP, EARLIER, PICK = CENTRE + 128, CENTRE + 256, CENTRE + 384, CENTRE + 512, CENTRE + 640
MASKS = PICK + E
TILE_NO = MASKS + 2 * LEVELS * T
SMALL = TILE_NO + 2 * B * CH
HALF, EPS, TINY, LNS, ONE, ROW, TINYSQ = range(SMALL, SMALL + 7)
NCONST = SMALL + 8
V_TOKB, V_BQ, V_BK, V_BV, V_BG, V_CW, V_CB, V_NORM, V_BO = 0, 1, 2, 3, 4, 5, 17, 20, 21
NVEC = 22
LN_SCALE = 2.0 ** 30
LAM = 1.0 / (1.0 + 1e-7)


def constants():
    c = np.zeros((128, NCONST), np.float32)
    i, j = np.indices((128, 128))
    c[:, IDENT:IDENT + 128] = i == j
    c[:T, TRI_LE:TRI_LE + T] = (i <= j)[:T, :T]
    c[:T, TRI_GT:TRI_GT + T] = (i > j)[:T, :T]
    c[:, BAND:BAND + T] = ((i >= j) & (i < j + TAPS))[:, :T]
    c[:, CENTRE:CENTRE + 128] = (i == j) - 1.0 / F
    c[:, MEAN:MEAN + 128] = 1.0 / F
    c[:, ONES:ONES + 128] = 1.0
    c[:, GROUP:GROUP + 128] = i // B == j // B
    c[:, EARLIER:EARLIER + 128] = (i // B == j // B) & (i < j)
    c[:, PICK:PICK + E] = (i == B * j)[:, :E]
    for m in range(LEVELS):
        s = 1 << m
        low = (i // (2 * s) == j // (2 * s)) & (i // s > j // s)
        at = MASKS + 2 * m * T
        c[:T, at:at + T] = low[:T, :T]
        c[:T, at + T:at + 2 * T] = low.T[:T, :T]
    c[:, TILE_NO:SMALL] = np.tile(np.add.outer(np.arange(CH), CH * np.arange(B)).ravel(), 2)
    c[:, HALF] = 0.5
    c[:, EPS] = 1e-5
    c[:, TINY] = 2.0 ** -62
    c[:, LNS] = 0.5 * np.log(LN_SCALE)
    c[:, ONE] = 1.0
    c[:, ROW] = np.arange(128)
    return c


def tower(nc, x, consts, vecs, wconv, wlin, wab, bab, wr, w1, b1, w2, b2, out, x2_rows, logits):
    f32, bf16, i32, u32 = mybir.dt.float32, mybir.dt.bfloat16, mybir.dt.int32, mybir.dt.uint32
    ACT = mybir.ActivationFunctionType
    X = mybir.AxisListType.X
    ctx = ExitStack()
    with ctx:
        banks = [ctx.enter_context(nc.psum_tensor(f"bank{i}", [128, 512], f32)) for i in range(8)]
        cst = ctx.enter_context(nc.sbuf_tensor("cst", [128, NCONST], f32))
        wr_sb = ctx.enter_context(nc.sbuf_tensor("wr_sb", [128, E], f32))
        tokens_phase(nc, banks, cst, wr_sb, x, consts, vecs, wconv, wlin, wab, bab, wr, out, x2_rows,
                     logits, f32, i32, ACT, X)
        experts_phase(nc, banks, cst, wr_sb, w1, b1, w2, b2, out, x2_rows, logits,
                      f32, bf16, i32, u32, ACT, X)


def tokens_phase(nc, banks, cst, wr_sb, x, consts, vecs, wconv, wlin, wab, bab, wr, out, x2_rows,
                 logits, f32, i32, ACT, X):
    ctx = ExitStack()
    with ctx:
        def sb(name, shape, dt=f32):
            return ctx.enter_context(nc.sbuf_tensor(name, shape, dt))

        def pair(name, shape):
            return [sb(f"{name}{q}", shape) for q in range(2)]

        def sem(name):
            return ctx.enter_context(nc.semaphore(name))

        def sems(name):
            return [sem(f"{name}{q}") for q in range(2)]

        vec = sb("vec", [128, NVEC])
        conv_w = sb("conv_w", [128, 5, F])
        lin_w = sb("lin_w", [128, 5, 128])
        ab_w = sb("ab_w", [128, 2])
        ab_b = sb("ab_b", [128, 2])
        xin = pair("xin", [XS, Q, 2 * CIN])
        xsq = pair("xsq", [XS, Q, CIN])
        ssq = pair("ssq", [XS, Q])
        xT = pair("xT", [128, Q, XR])
        wcol = pair("wcol", [T, Q])
        scl = pair("scl", [128, W])
        hT = pair("hT", [128, W])
        sqr = pair("sqr", [128, W])
        rstd = pair("rstd", [128, W])
        xn = pair("xn", [128, W])
        lin = [pair(f"lin{j}", [128, Q, T + HALO]) for j in range(3)]
        gate = pair("gate", [128, W])
        act = [pair(f"act{j}", [128, W]) for j in range(3)]
        zab = pair("zab", [T, Q, 2])
        nab = pair("nab", [T, Q, 2])
        eab = pair("eab", [T, Q, 2])
        gab = pair("gab", [T, Q, 2])
        beta = pair("beta", [T, Q])
        sq2 = pair("sq2", [128, W])
        rq = pair("rq", [128, W])
        kg = pair("kg", [128, W])
        qg = pair("qg", [128, W])
        gl = pair("gl", [T, W])
        dec = pair("dec", [T, W])
        eg = pair("eg", [128, W])
        eb = pair("eb", [T, W])
        ua = pair("ua", [T, W])
        pt = pair("pt", [T, W])
        inv = pair("inv", [T, W])
        invT = pair("invT", [T, W])
        ps = pair("ps", [T, W])
        rhs = pair("rhs", [T, Q * 128])
        u = pair("u", [T, Q * 128])
        ue = pair("ue", [T, Q * 128])
        kN = pair("kN", [T, Q * 128])
        st = pair("st", [128, Q * 128])
        h2N = pair("h2N", [T, Q * 128])
        x2N = pair("x2N", [T, Q * 128])
        lg = pair("lg", [E, W])

        S, PLACE = {}, {}
        for names in ("xin_loaded", "xsq_done", "ssq_done", "xT_ready wsum_ready conv_ready scale_ready",
                      "xT_done scale_done tanh_done", "wmax_done wroot_done weps_done wrec_done wcol_done",
                      "v_done h_done xn_done", "xm_ready var_ready om_ready ovar_ready h2m_ready h2var_ready",
                      "xmsq_done osq_done h2sq_done",
                      "lnv_done rstd_done lnk_done rk_done lno_done rstdo_done lnh2_done rstdh2_done",
                      "linq_ready link_ready linv_ready gab_ready", "linq_done link_done linv_done",
                      "zab_done gatelin_done", "halo_done", "tap0_done", "tap_done",
                      "z_done nz_done az_done mab_done g_done", "eab_done lab_done beta_done", "silu_done",
                      "sqqk_done", "nq_ready nk_ready", "lnq_done rq_done", "qn_done kn_done kg_done",
                      "gl_done", "D_ready cum_ready", "edec_done eg_done", "dec_done nbeta_done eb_done",
                      "qg_done", "kk_ready kq_ready kN_ready R_ready", "ua_done pt_done", "kN_done",
                      "rhs_done", "eye_done", "P_ready", "P_done", "XPX_ready", "inv_done", "YPY_ready",
                      "invT_done", "W_ready O_ready dS_ready", "u_done", "ue_done", "O_done",
                      "decay_st_done", "st_done", "on_done gated_done h2_done x2_done",
                      "y_ready lg_ready x2N_ready h2N_ready", "lg_done h2N_done", "x2N_done",
                      "lg_stored", "h2_stored", "x2_stored"):
            order = names.split()
            shared = sems(order[0] if len(order) == 1 else f"{order[0]}_to_{order[-1]}")
            for k, name in enumerate(order):
                S[name], PLACE[name] = shared, (len(order), k + 1)

        AHEAD = {"xsq_done": 1, "ssq_done": 1, "scale_ready": 1, "x2_done": 1, "h2N_done": 1, "x2N_done": 1,
                 "silu_done": 1, "tap_done": 1, "dS_ready": 1, "lg_stored": 16, "h2_stored": 16,
                 "x2_stored": 16}
        ahead = {id(S[name]): by for name, by in AHEAD.items()}

        def count(name, turn):
            per, at = PLACE[name]
            return turn * per - (per - at) + ahead.get(id(S[name]), 0)

        def give_ahead(eng, *names):
            for name in names:
                for q in range(2):
                    eng.sem_inc(S[name][q], AHEAD[name])

        weights_loaded = sem("weights_loaded")

        def bank(q, i):
            return banks[4 * q + i]

        def over(ap, width=T):
            return ap.unsqueeze(1).to_broadcast([ap.shape[0], Q, width])

        def along(ap, width):
            return ap.unsqueeze(2).to_broadcast([ap.shape[0], Q, width])

        def tiles(buf, width=T):
            return buf[:, :].rearrange("p (i t) -> p i t", i=Q) if width == T else \
                buf[:, :].rearrange("p (i d) -> p i d", i=Q)

        def c(at, rows, cols):
            return cst[0:rows, at:at + cols]

        def v(at):
            return vec[:, at:at + 1]

        NW = 8
        qc = {"q": 0, "k": 1, "v": 2}
        x_t = x.rearrange("b t c -> t b c")
        out_t = out.rearrange("b t f -> t b f")
        x2_t = x2_rows.rearrange("(b t) f -> t b f", b=B)

        with nc.Block() as block:

            @block.sync
            def _(sp):
                sp.dma_start(cst[:, :], consts).then_inc(weights_loaded, 16)
                sp.dma_start(vec[:, :], vecs).then_inc(weights_loaded, 16)
                sp.dma_start(conv_w[:, 0:4, :], wconv[0:512, :].rearrange("(k p) f -> p k f", k=4))\
                    .then_inc(weights_loaded, 16)
                sp.dma_start(conv_w[64:128, 4, :], wconv[512:576, :]).then_inc(weights_loaded, 16)
                sp.dma_start(lin_w[:, :, :], wlin.rearrange("k p f -> p k f")).then_inc(weights_loaded, 16)
                sp.dma_start(ab_w[:, :], wab).then_inc(weights_loaded, 16)
                sp.dma_start(ab_b[:, :], bab.partition_broadcast(128)).then_inc(weights_loaded, 16)
                sp.dma_start(wr_sb[:, :], wr).then_inc(weights_loaded, 16)
                give_ahead(sp, "lg_stored", "h2_stored", "x2_stored")
                with sp.Fori(0, OCT) as o:
                    with sp.Fori(0, CH) as ch:
                        n = sp.snap(o * CH + ch)
                        seqs = [sp.snap(o * (2 * Q) + q * Q) for q in range(2)]
                        for q in range(2):
                            rows = [x_t[bass.ds(ch * T + s, XS - s), bass.ds(seqs[q], Q), :] for s in range(2)]
                            squared, transposed = sp.to_reg(sp.snap(count("xsq_done", n))), sp.to_reg(sp.snap(count("scale_ready", n)))
                            sp.wait_ge(S["xsq_done"][q], squared)
                            sp.wait_ge(S["scale_ready"][q], transposed)
                            for s in range(2):
                                sp.dma_start(xin[q][0:XS - s, :, s * CIN:(s + 1) * CIN], rows[s])\
                                    .then_inc(S["xin_loaded"][q], 16)
                        for q in range(2):
                            here = (bass.ds(ch * T, T), bass.ds(seqs[q], Q))
                            sp.wait_ge(S["lg_done"][q], count("lg_done", n + 1))
                            sp.dma_start(logits[:, here[1], here[0]],
                                         lg[q][:, :].rearrange("e (i t) -> e i t", i=Q)).then_inc(S["lg_stored"][q], 16)
                            sp.wait_ge(S["h2N_done"][q], count("h2N_done", n + 1))
                            sp.dma_start(out_t[here[0], here[1], :], tiles(h2N[q], 128)).then_inc(S["h2_stored"][q], 16)
                            sp.wait_ge(S["x2N_done"][q], count("x2N_done", n + 1))
                            sp.dma_start(x2_t[here[0], here[1], :], tiles(x2N[q], 128)).then_inc(S["x2_stored"][q], 16)
                for q in range(2):
                    for k in ("lg_stored", "h2_stored", "x2_stored"):
                        sp.wait_ge(S[k][q], 16 * OCT * CH + 16)

            @block.tensor
            def _(pe):
                def bmm(dst, lhs, rhs_, width, sem_, q):
                    for i in range(Q):
                        m = nc.tensor.matmul(dst(i), lhs(i), rhs_(i), start=True, stop=True)
                    m.then_inc(S[sem_][q], 1)

                def t(buf, q, i):
                    return buf[q][:, i * T:(i + 1) * T]

                def d(buf, q, i):
                    return buf[q][:, i * 128:(i + 1) * 128]

                def pT(q, b, i, rows=T):
                    return bank(q, b)[0:rows, i * T:(i + 1) * T]

                def pD(q, b, i, rows=T):
                    return bank(q, b)[0:rows, i * 128:(i + 1) * 128]

                pe.wait_ge(weights_loaded, 16 * NW)
                give_ahead(pe, "scale_ready", "dS_ready")
                with pe.Fori(0, OCT) as o:
                    with pe.Fori(0, CH) as ch:
                        n = o * CH + ch
                        now = n + 1

                        def wait(name, q, k=None):
                            pe.wait_ge(S[name][q], count(name, now) if k is None else k)

                        for q in range(2):
                            wait("xin_loaded", q, 32 * now)
                            wait("x2_done", q, count("x2_done", n))
                            for i in range(Q):
                                m = nc.tensor.transpose(bank(q, 0)[:, i * XR:(i + 1) * XR], xin[q][0:XR, i, :],
                                                        c(IDENT, XR, XR))
                            m.then_inc(S["xT_ready"][q], 1)
                        for q in range(2):
                            wait("ssq_done", q)
                            wait("h2N_done", q, count("h2N_done", n))
                            nc.tensor.matmul(bank(q, 2)[0:T, 0:Q], c(BAND, XS, T), ssq[q][:, :],
                                             start=True, stop=True).then_inc(S["wsum_ready"][q], 1)
                            wait("xT_done", q)
                            wait("x2N_done", q, n + 1)
                            for k in range(5):
                                p0 = 64 if k == 4 else 0
                                at = 2 * k if k < 4 else TAPS - 2
                                m = nc.tensor.matmul(bank(q, 1)[:, 0:W], conv_w[p0:128, k, :],
                                                     xT[q][p0:128, :, at:at + T],
                                                     start=(k == 0), stop=(k == 4))
                            m.then_inc(S["conv_ready"][q], 1)
                        for q in range(2):
                            wait("wcol_done", q)
                            bmm(lambda i: pT(q, 2, i, 128),
                                lambda i: wcol[q][:, i:i + 1].to_broadcast([T, 128]),
                                lambda i: c(IDENT, T, T), T, "scale_ready", q)

                        def centre(q, src, b, done, ready):
                            wait(done, q)
                            nc.tensor.matmul(bank(q, b)[:, 0:W], c(CENTRE, 128, 128), src[q][:, :],
                                             start=True, stop=True).then_inc(S[ready][q], 1)

                        def variance(q, b, done, ready):
                            wait(done, q)
                            nc.tensor.matmul(bank(q, b)[:, 0:W], c(MEAN, 128, 128), sqr[q][:, :],
                                             start=True, stop=True).then_inc(S[ready][q], 1)

                        for q in range(2):
                            centre(q, hT, 0, "h_done", "xm_ready")
                        for q in range(2):
                            wait("h2N_done", q, count("h2N_done", n))
                            variance(q, 3, "xmsq_done", "var_ready")
                        for q in range(2):
                            wait("xn_done", q)
                            for j, ready in enumerate(("linq_ready", "link_ready", "linv_ready")):
                                nc.tensor.matmul(bank(q, 1 + j)[:, 0:W], lin_w[:, j, :], xn[q][:, :],
                                                 start=True, stop=True).then_inc(S[ready][q], 1)
                            nc.tensor.matmul(bank(q, 0)[:, 0:W], lin_w[:, 3, :], xn[q][:, :],
                                             start=True, stop=True)
                            bmm(lambda i: bank(q, 0)[0:T, W + 2 * i:W + 2 * i + 2],
                                lambda i: t(xn, q, i), lambda i: ab_w[:, :], 2, "gab_ready", q)
                        for q in range(2):
                            wait("sqqk_done", q)
                            nc.tensor.matmul(bank(q, 1)[:, 0:W], c(ONES, 128, 128), sqr[q][:, :],
                                             start=True, stop=True).then_inc(S["nq_ready"][q], 1)
                            nc.tensor.matmul(bank(q, 2)[:, 0:W], c(ONES, 128, 128), sq2[q][:, :],
                                             start=True, stop=True).then_inc(S["nk_ready"][q], 1)
                        for q in range(2):
                            wait("gl_done", q)
                            wait("linv_done", q)
                            nc.tensor.matmul(bank(q, 3)[0:T, 0:W], c(TRI_GT, T, T), gl[q][:, :],
                                             start=True, stop=True).then_inc(S["D_ready"][q], 1)
                            wait("gatelin_done", q)
                            nc.tensor.matmul(bank(q, 0)[:, 0:W], c(ONES, T, 128), gl[q][:, :],
                                             start=True, stop=True).then_inc(S["cum_ready"][q], 1)
                        for q in range(2):
                            wait("kn_done", q)
                            bmm(lambda i: pT(q, 1, i), lambda i: t(act[1], q, i), lambda i: t(act[1], q, i),
                                T, "kk_ready", q)
                            bmm(lambda i: pT(q, 2, i), lambda i: t(act[1], q, i), lambda i: t(act[0], q, i),
                                T, "kq_ready", q)
                            wait("edec_done", q)
                            for i in range(Q):
                                m = nc.tensor.transpose(pD(q, 3, i), t(act[1], q, i), c(IDENT, 128, 128))
                            m.then_inc(S["kN_ready"][q], 1)
                        for q in range(2):
                            wait("kg_done", q)
                            wait("st_done", q, n + o + 1)
                            for i in range(Q):
                                nc.tensor.matmul(pD(q, 0, i), t(act[2], q, i), c(IDENT, 128, 128),
                                                 start=True, stop=False)
                                m = nc.tensor.matmul(pD(q, 0, i), t(kg, q, i), d(st, q, i),
                                                     start=False, stop=True)
                            m.then_inc(S["R_ready"][q], 1)
                        for q in range(2):
                            wait("ua_done", q)
                            for i in range(Q):
                                m = nc.tensor.transpose(pT(q, 1, i), t(ua, q, i), c(IDENT, T, T))
                            m.then_inc(S["P_ready"][q], 1)
                        for lev in range(1, LEVELS):
                            for q in range(2):
                                wait("inv_done", q, n * (LEVELS - 1) + lev)
                                if lev > 1:
                                    wait("P_done", q, n * (LEVELS - 1) + lev - 1)
                                bmm(lambda i: pT(q, 1, i), lambda i: t(ua, q, i), lambda i: t(inv, q, i),
                                    T, "P_ready", q)
                            for q in range(2):
                                wait("P_done", q, n * (LEVELS - 1) + lev)
                                wait("invT_done", q, n * LEVELS + lev)
                                if lev < LEVELS - 1:
                                    if lev == 1:
                                        wait("pt_done", q)
                                    bmm(lambda i: pT(q, 2, i), lambda i: t(invT, q, i), lambda i: t(ps, q, i),
                                        T, "XPX_ready", q)
                                if lev == 1:
                                    wait("kN_done", q)
                                bmm(lambda i: pT(q, 3, i), lambda i: t(ps, q, i), lambda i: t(invT, q, i),
                                    T, "YPY_ready", q)
                        for q in range(2):
                            wait("invT_done", q, n * LEVELS + LEVELS)
                            wait("rhs_done", q)
                            bmm(lambda i: pD(q, 1, i), lambda i: t(invT, q, i), lambda i: d(rhs, q, i),
                                128, "W_ready", q)
                        for q in range(2):
                            wait("qg_done", q)
                            wait("u_done", q)
                            for i in range(Q):
                                nc.tensor.matmul(pT(q, 2, i, 128), d(st, q, i), t(qg, q, i),
                                                 start=True, stop=False)
                                m = nc.tensor.matmul(pT(q, 2, i, 128), d(u, q, i), t(pt, q, i),
                                                     start=False, stop=True)
                            m.then_inc(S["O_ready"][q], 1)
                            wait("ue_done", q)
                            bmm(lambda i: pD(q, 0, i, 128), lambda i: d(kN, q, i), lambda i: d(ue, q, i),
                                128, "dS_ready", q)
                        for q in range(2):
                            centre(q, xn, 1, "O_done", "om_ready")
                        for q in range(2):
                            variance(q, 3, "osq_done", "ovar_ready")
                        for q in range(2):
                            wait("gated_done", q)
                            nc.tensor.matmul(bank(q, 2)[:, 0:W], lin_w[:, 4, :], xn[q][:, :],
                                             start=True, stop=True).then_inc(S["y_ready"][q], 1)
                        for q in range(2):
                            wait("st_done", q, n + o + 2)
                            centre(q, hT, 0, "h2_done", "h2m_ready")
                        for q in range(2):
                            variance(q, 3, "h2sq_done", "h2var_ready")
                        for q in range(2):
                            wait("x2_done", q)
                            nc.tensor.matmul(bank(q, 2)[0:E, 0:W], wr_sb[:, :], xn[q][:, :],
                                             start=True, stop=True).then_inc(S["lg_ready"][q], 1)
                            for i in range(Q):
                                m = nc.tensor.transpose(pD(q, 1, i), t(xn, q, i), c(IDENT, 128, 128))
                            m.then_inc(S["x2N_ready"][q], 1)
                            for i in range(Q):
                                m = nc.tensor.transpose(pD(q, 3, i), t(hT, q, i), c(IDENT, 128, 128))
                            m.then_inc(S["h2N_ready"][q], 1)

            @block.scalar
            def _(sc):
                sc.wait_ge(weights_loaded, 16 * NW)
                give_ahead(sc, "h2N_done", "silu_done")
                with sc.Fori(0, OCT) as o:
                    with sc.Fori(0, CH) as ch:
                        n = o * CH + ch
                        now = n + 1

                        def wait(name, q, k=None):
                            sc.wait_ge(S[name][q], count(name, now) if k is None else k)

                        def act_(done, q, dst, src, fn, **kw):
                            nc.scalar.activation(dst, src, fn, **kw).then_inc(S[done][q], 1)

                        for q in range(2):
                            wait("xT_ready", q)
                            act_("xT_done", q, xT[q][:, :, :],
                                 bank(q, 0)[:, 0:Q * XR].rearrange("p (i t) -> p i t", i=Q), ACT.Copy)
                        for q in range(2):
                            wait("scale_ready", q)
                            act_("scale_done", q, scl[q][:, :], bank(q, 2)[:, 0:W], ACT.Copy)
                        for q in range(2):
                            wait("v_done", q)
                            act_("tanh_done", q, hT[q][:, :], scl[q][:, :], ACT.Tanh, scale=LAM)
                        for q in range(2):
                            wait("xm_ready", q)
                            act_("xmsq_done", q, sqr[q][:, :], bank(q, 0)[:, 0:W], ACT.Square)

                        def inverse_root(q, b, ready, ln, root):
                            wait(ready, q)
                            act_(ln, q, rstd[q][:, :], bank(q, b)[:, 0:W], ACT.Ln, bias=c(EPS, 128, 1))
                            wait(ln, q)
                            act_(root, q, rstd[q][:, :], rstd[q][:, :], ACT.Exp, scale=-0.5)

                        for q in range(2):
                            inverse_root(q, 3, "var_ready", "lnv_done", "rstd_done")
                        for q in range(2):
                            for j, name in enumerate(("linq", "link", "linv")):
                                wait(name + "_ready", q)
                                if j == 0:
                                    wait("halo_done", q, now + o)
                                act_(name + "_done", q, lin[j][q][:, :, HALO:HALO + T],
                                     bank(q, 1 + j)[:, 0:W].rearrange("p (i t) -> p i t", i=Q),
                                     ACT.Identity, bias=v(V_BQ + j))
                            wait("gab_ready", q)
                            act_("zab_done", q, zab[q][:, :, :],
                                 bank(q, 0)[0:T, W:W + 2 * Q].rearrange("p (i a) -> p i a", i=Q), ACT.Copy)
                            act_("gatelin_done", q, gate[q][:, :], bank(q, 0)[:, 0:W], ACT.Silu, bias=v(V_BG))
                        for q in range(2):
                            for j in range(3):
                                wait("tap_done", q, (3 * n + j + 1) * HALO + 1)
                                act_("silu_done", q, act[j][q][:, :], act[j][q][:, :], ACT.Silu)
                        for q in range(2):
                            wait("az_done", q)
                            act_("eab_done", q, eab[q][:, :, :], eab[q][:, :, :], ACT.Exp, scale=-1.0)
                            wait("eab_done", q)
                            act_("lab_done", q, eab[q][:, :, :], eab[q][:, :, :], ACT.Ln, bias=1.0)
                            wait("g_done", q)
                            act_("beta_done", q, beta[q][:, :], gab[q][:, :, 1], ACT.Exp)
                        for q in range(2):
                            wait("nq_ready", q)
                            act_("lnq_done", q, rq[q][:, :], bank(q, 1)[:, 0:W], ACT.Ln,
                                 scale=LN_SCALE, bias=c(TINY, 128, 1))
                            wait("nk_ready", q)
                            act_("lnk_done", q, rstd[q][:, :], bank(q, 2)[:, 0:W], ACT.Ln,
                                 scale=LN_SCALE, bias=c(TINY, 128, 1))
                            wait("lnq_done", q)
                            act_("rq_done", q, rq[q][:, :], rq[q][:, :], ACT.Exp, scale=-0.5, bias=c(LNS, 128, 1))
                            wait("lnk_done", q)
                            act_("rk_done", q, rstd[q][:, :], rstd[q][:, :], ACT.Exp, scale=-0.5,
                                 bias=c(LNS, 128, 1))
                        for q in range(2):
                            wait("D_ready", q)
                            act_("edec_done", q, dec[q][:, :], bank(q, 3)[0:T, 0:W], ACT.Exp)
                            wait("cum_ready", q)
                            act_("eg_done", q, eg[q][:, :], bank(q, 0)[:, 0:W], ACT.Exp)
                        for q in range(2):
                            wait("kN_ready", q)
                            act_("kN_done", q, kN[q][:, :], bank(q, 3)[0:T, :], ACT.Copy)
                        for q in range(2):
                            wait("R_ready", q)
                            act_("rhs_done", q, rhs[q][:, :], bank(q, 0)[0:T, :], ACT.Copy)
                        for lev in range(1, LEVELS):
                            for q in range(2):
                                wait("P_ready", q, n * LEVELS + lev + 1)
                                act_("P_done", q, ps[q][:, :], bank(q, 1)[0:T, 0:W], ACT.Copy)
                        for q in range(2):
                            wait("O_ready", q)
                            act_("O_done", q, xn[q][:, :], bank(q, 2)[:, 0:W], ACT.Copy)
                        for q in range(2):
                            wait("om_ready", q)
                            act_("osq_done", q, sqr[q][:, :], bank(q, 1)[:, 0:W], ACT.Square)
                        for q in range(2):
                            inverse_root(q, 3, "ovar_ready", "lno_done", "rstdo_done")
                        for q in range(2):
                            wait("h2m_ready", q)
                            act_("h2sq_done", q, sqr[q][:, :], bank(q, 0)[:, 0:W], ACT.Square)
                        for q in range(2):
                            inverse_root(q, 3, "h2var_ready", "lnh2_done", "rstdh2_done")
                        for q in range(2):
                            wait("lg_ready", q)
                            wait("lg_stored", q, 16 * n + 16)
                            act_("lg_done", q, lg[q][:, :], bank(q, 2)[0:E, 0:W], ACT.Copy)
                            wait("h2N_ready", q)
                            wait("h2_stored", q, 16 * n + 16)
                            act_("h2N_done", q, h2N[q][:, :], bank(q, 3)[0:T, :], ACT.Copy)

            @block.vector
            def _(ve):
                ve.wait_ge(weights_loaded, 16 * NW)
                give_ahead(ve, "ssq_done", "x2_done", "x2N_done", "tap_done")
                with ve.Fori(0, OCT) as o:
                    for q in range(2):
                        ve.wait_ge(S["dS_ready"][q], count("dS_ready", o * CH))
                        nc.vector.memset(st[q][:, :], 0.0).then_inc(S["st_done"][q], 1)
                    with ve.Fori(0, CH) as ch:
                        n = o * CH + ch
                        now = n + 1

                        def wait(name, q, k=None):
                            ve.wait_ge(S[name][q], count(name, now) if k is None else k)

                        def wait_each(q, *signals):
                            values = [(name, ve.to_reg(ve.snap(count(name, now) if k is None else k)))
                                      for name, k in signals]
                            ve.wait_ge(weights_loaded, 16 * NW)
                            for name, value in values:
                                ve.wait_ge(S[name][q], value)

                        def inc(ins, name, q):
                            ins.then_inc(S[name][q], 1)

                        for q in range(2):
                            wait("xsq_done", q)
                            inc(nc.vector.reduce_sum(ssq[q][:, :], xsq[q][:, :, :], X), "ssq_done", q)
                        for q in range(2):
                            wait("wsum_ready", q)
                            inc(nc.vector.tensor_scalar(wcol[q][:, :], bank(q, 2)[0:T, 0:Q], 0.0, None, ALU.max),
                                "wmax_done", q)
                        for q in range(2):
                            wait("wroot_done", q)
                            inc(nc.vector.tensor_scalar(wcol[q][:, :], wcol[q][:, :], 1e-7, None, ALU.add),
                                "weps_done", q)
                        for q in range(2):
                            wait("weps_done", q)
                            inc(nc.vector.reciprocal(wcol[q][:, :], wcol[q][:, :]), "wrec_done", q)
                        for q in range(2):
                            wait("wrec_done", q)
                            inc(nc.vector.tensor_scalar(wcol[q][:, :], wcol[q][:, :], 1.0, None, ALU.min),
                                "wcol_done", q)
                        for q in range(2):
                            wait("conv_ready", q)
                            wait("scale_done", q)
                            inc(nc.vector.tensor_tensor(scl[q][:, :], bank(q, 1)[:, 0:W], scl[q][:, :], ALU.mult),
                                "v_done", q)
                        for q in range(2):
                            wait("tanh_done", q)
                            inc(nc.vector.tensor_scalar(hT[q][:, :], hT[q][:, :], v(V_TOKB), 0.0, ALU.add, ALU.max),
                                "h_done", q)
                        for q in range(2):
                            wait("rstd_done", q)
                            inc(nc.vector.tensor_tensor(xn[q][:, :], bank(q, 0)[:, 0:W], rstd[q][:, :], ALU.mult),
                                "xn_done", q)
                        for q in range(2):
                            wait("zab_done", q)
                            inc(nc.vector.tensor_tensor(zab[q][:, :, :], zab[q][:, :, :],
                                                        over(ab_b[0:T, :], 2), ALU.add), "z_done", q)
                            wait("z_done", q)
                            inc(nc.vector.tensor_scalar(nab[q][:, :, :], zab[q][:, :, :], -1.0, None, ALU.mult),
                                "nz_done", q)
                            wait("nz_done", q)
                            inc(nc.vector.tensor_tensor(eab[q][:, :, :], zab[q][:, :, :], nab[q][:, :, :], ALU.max),
                                "az_done", q)
                            wait("az_done", q)
                            inc(nc.vector.tensor_scalar(nab[q][:, :, :], zab[q][:, :, :], 0.0, None, ALU.min),
                                "mab_done", q)
                        for j, name in enumerate("qkv"):
                            for q in range(2):
                                for k in range(1, DW):
                                    if k == 1:
                                        wait("tap0_done", q, 3 * n + j + 1)
                                    else:
                                        wait("tap_done", q, (3 * n + j) * HALO + k)
                                    inc(nc.vector.scalar_tensor_tensor(
                                        tiles(act[j][q]), lin[j][q][:, :, k:k + T], v(V_CW + DW * j + k),
                                        tiles(act[j][q]), ALU.mult, ALU.add), "tap_done", q)
                        for q in range(2):
                            wait("lab_done", q)
                            wait("mab_done", q)
                            inc(nc.vector.tensor_tensor(gab[q][:, :, :], nab[q][:, :, :], eab[q][:, :, :],
                                                        ALU.subtract), "g_done", q)
                        for q in range(2):
                            wait("rq_done", q)
                            inc(nc.vector.scalar_tensor_tensor(act[0][q][:, :], rq[q][:, :], 1e12,
                                                               act[0][q][:, :], ALU.min, ALU.mult), "qn_done", q)
                            wait("rk_done", q)
                            inc(nc.vector.scalar_tensor_tensor(act[1][q][:, :], rstd[q][:, :], 1e12,
                                                               act[1][q][:, :], ALU.min, ALU.mult), "kn_done", q)
                            wait("kn_done", q)
                            wait("eg_done", q)
                            inc(nc.vector.scalar_tensor_tensor(kg[q][:, :], act[1][q][:, :], -1.0, eg[q][:, :],
                                                               ALU.mult, ALU.mult), "kg_done", q)
                        for q in range(2):
                            wait("kk_ready", q)
                            wait("eb_done", q)
                            inc(nc.vector.tensor_tensor(ua[q][:, :], bank(q, 1)[0:T, 0:W], eb[q][:, :], ALU.mult),
                                "ua_done", q)
                            wait("kq_ready", q)
                            inc(nc.vector.tensor_tensor(pt[q][:, :], bank(q, 2)[0:T, 0:W], dec[q][:, :], ALU.mult),
                                "pt_done", q)

                        def mask(lev, side):
                            return over(c(MASKS + (2 * lev + side) * T, T, T)).bitcast(i32)

                        for q in range(2):
                            wait_each(q, ("ua_done", None), ("eye_done", None))
                            inc(nc.vector.copy_predicated(tiles(invT[q]), mask(0, 1), tiles(ua[q])), "invT_done", q)
                            wait_each(q, ("P_ready", n * LEVELS + 1))
                            inc(nc.vector.copy_predicated(
                                tiles(inv[q]), mask(0, 0),
                                bank(q, 1)[0:T, 0:W].rearrange("p (i t) -> p i t", i=Q)), "inv_done", q)
                        for lev in range(1, LEVELS):
                            for q in range(2):
                                if lev < LEVELS - 1:
                                    wait_each(q, ("XPX_ready", n * (LEVELS - 2) + lev))
                                    inc(nc.vector.copy_predicated(
                                        tiles(inv[q]), mask(lev, 0),
                                        bank(q, 2)[0:T, 0:W].rearrange("p (i t) -> p i t", i=Q)), "inv_done", q)
                                wait_each(q, ("YPY_ready", n * (LEVELS - 1) + lev))
                                inc(nc.vector.copy_predicated(
                                    tiles(invT[q]), mask(lev, 1),
                                    bank(q, 3)[0:T, 0:W].rearrange("p (i t) -> p i t", i=Q)), "invT_done", q)
                        for q in range(2):
                            wait("W_ready", q)
                            inc(nc.vector.tensor_tensor(tiles(u[q], 128),
                                                        bank(q, 1)[0:T, :].rearrange("p (i d) -> p i d", i=Q),
                                                        along(beta[q][:, :], 128), ALU.mult), "u_done", q)
                        for q in range(2):
                            wait("decay_st_done", q)
                            wait("dS_ready", q)
                            inc(nc.vector.tensor_tensor(st[q][:, :], bank(q, 0)[:, :], st[q][:, :], ALU.add),
                                "st_done", q)
                        for q in range(2):
                            wait("rstdo_done", q)
                            inc(nc.vector.tensor_tensor(xn[q][:, :], bank(q, 1)[:, 0:W], rstd[q][:, :], ALU.mult),
                                "on_done", q)
                            wait("on_done", q)
                            inc(nc.vector.scalar_tensor_tensor(xn[q][:, :], xn[q][:, :], v(V_NORM), gate[q][:, :],
                                                               ALU.mult, ALU.mult), "gated_done", q)
                        for q in range(2):
                            wait("y_ready", q)
                            inc(nc.vector.scalar_tensor_tensor(hT[q][:, :], bank(q, 2)[:, 0:W], v(V_BO),
                                                               hT[q][:, :], ALU.add, ALU.add), "h2_done", q)
                        for q in range(2):
                            wait("rstdh2_done", q)
                            inc(nc.vector.tensor_tensor(xn[q][:, :], bank(q, 0)[:, 0:W], rstd[q][:, :], ALU.mult),
                                "x2_done", q)
                        for q in range(2):
                            wait("x2N_ready", q)
                            wait("x2_stored", q, 16 * n + 16)
                            inc(nc.vector.tensor_copy(x2N[q][:, :], bank(q, 1)[0:T, :]), "x2N_done", q)

            @block.gpsimd
            def _(po):
                po.wait_ge(weights_loaded, 16 * NW)
                give_ahead(po, "xsq_done")
                with po.Fori(0, OCT) as o:
                    for q in range(2):
                        moved = po.to_reg(po.snap(o * (CH * 3 * HALO) + 1))
                        po.wait_ge(weights_loaded, 16 * NW)
                        po.wait_ge(S["tap_done"][q], moved)
                        for j in range(3):
                            ins = nc.gpsimd.memset(lin[j][q][:, :, 0:HALO], 0.0)
                        ins.then_inc(S["halo_done"][q], 1)
                    with po.Fori(0, CH) as ch:
                        n = o * CH + ch
                        now = n + 1

                        def wait(name, q, k=None):
                            po.wait_ge(S[name][q], count(name, now) if k is None else k)

                        def wait_each(q, *signals):
                            values = [(name, po.to_reg(po.snap(count(name, now) if k is None else k)))
                                      for name, k in signals]
                            po.wait_ge(weights_loaded, 16 * NW)
                            for name, value in values:
                                po.wait_ge(S[name][q], value)

                        def inc(ins, name, q):
                            ins.then_inc(S[name][q], 1)

                        for q in range(2):
                            wait("xin_loaded", q, 32 * now)
                            wait("ssq_done", q, n + 1)
                            inc(nc.gpsimd.tensor_tensor(xsq[q][:, :, :], xin[q][:, :, 0:CIN], xin[q][:, :, 0:CIN],
                                                        ALU.mult), "xsq_done", q)
                        for q in range(2):
                            wait("wmax_done", q)
                            inc(nc.gpsimd.tensor_tensor(wcol[q][:, :], wcol[q][:, :],
                                                        c(HALF, T, 1).to_broadcast([T, Q]), ALU.pow),
                                "wroot_done", q)
                        for j, name in enumerate(("linq", "link", "linv")):
                            for q in range(2):
                                wait_each(q, (name + "_done", None), ("silu_done", 3 * n + 1))
                                inc(nc.gpsimd.tensor_scalar(tiles(act[j][q]), lin[j][q][:, :, 0:T],
                                                            v(V_CW + DW * j), v(V_CB + j), ALU.mult, ALU.add),
                                    "tap0_done", q)
                        for q in range(2):
                            wait("silu_done", q, 3 * n + 3)
                            nc.gpsimd.tensor_tensor(sqr[q][:, :], act[0][q][:, :], act[0][q][:, :], ALU.mult)
                            inc(nc.gpsimd.tensor_tensor(sq2[q][:, :], act[1][q][:, :], act[1][q][:, :], ALU.mult),
                                "sqqk_done", q)
                        for q in range(2):
                            wait("g_done", q)
                            inc(nc.gpsimd.tensor_tensor(tiles(gl[q]), over(c(TRI_LE, T, T)),
                                                        along(gab[q][:, :, 0], T), ALU.mult), "gl_done", q)
                        for q in range(2):
                            wait("edec_done", q)
                            inc(nc.gpsimd.tensor_tensor(tiles(dec[q]), tiles(dec[q]), over(c(TRI_LE, T, T)),
                                                        ALU.mult), "dec_done", q)
                            wait_each(q, ("beta_done", None))
                            inc(nc.gpsimd.tensor_scalar(wcol[q][:, :], beta[q][:, :], -1.0, 0.0, ALU.mult, ALU.add),
                                "nbeta_done", q)
                            wait("dec_done", q)
                            wait("nbeta_done", q)
                            inc(nc.gpsimd.tensor_tensor(tiles(eb[q]), tiles(dec[q]), along(wcol[q][:, :], T),
                                                        ALU.mult), "eb_done", q)
                            wait("qn_done", q)
                            wait("eg_done", q)
                            inc(nc.gpsimd.tensor_tensor(qg[q][:, :], act[0][q][:, :], eg[q][:, :], ALU.mult),
                                "qg_done", q)
                            for k in (inv, invT):
                                ins = nc.gpsimd.tensor_scalar(tiles(k[q]), over(c(IDENT, T, T)), 1.0, 0.0,
                                                              ALU.mult, ALU.add)
                            inc(ins, "eye_done", q)
                        for q in range(2):
                            wait_each(q, ("tap_done", 3 * HALO * now + 1))
                            for j in range(3):
                                ins = nc.gpsimd.tensor_copy(lin[j][q][:, :, 0:HALO], lin[j][q][:, :, T:T + HALO])
                            inc(ins, "halo_done", q)
                        for q in range(2):
                            wait("u_done", q)
                            inc(nc.gpsimd.tensor_tensor(tiles(ue[q], 128), tiles(u[q], 128),
                                                        along(tiles(dec[q])[:, :, T - 1], 128), ALU.mult),
                                "ue_done", q)
                            wait("O_ready", q)
                            inc(nc.gpsimd.tensor_tensor(tiles(st[q], 128), tiles(st[q], 128),
                                                        along(tiles(eg[q])[:, :, T - 1], 128), ALU.mult),
                                "decay_st_done", q)


def experts_phase(nc, banks, cst, wr_sb, w1, b1, w2, b2, out, x2_rows, logits,
                  f32, bf16, i32, u32, ACT, X):
    PAIRS = E // 2
    FC = FF // 128
    TB = CH * B
    PX = 2 * TB
    ROUNDS = 31
    HALF_T = ST // 2
    ctx = ExitStack()
    with ctx:
        def sb(name, shape, dt=f32):
            return ctx.enter_context(nc.sbuf_tensor(name, shape, dt))

        def sem(name):
            return ctx.enter_context(nc.semaphore(name))

        lgt = sb("lgt", [128, L])
        dist = sb("dist", [128, L])
        scan_one = sb("scan_one", [128, L])
        work = sb("work", [128, L])
        below = sb("below", [128, L])
        ties = sb("ties", [128, L])
        chosen = sb("chosen", [128, L])
        slot = sb("slot", [128, L])
        sloti = sb("sloti", [128, L], i32)
        hii = sb("hii", [128, L], i32)
        loi = sb("loi", [128, L], i32)
        hib = sb("hib", [128, L], bf16)
        lob = sb("lob", [128, L], bf16)
        rowmax = sb("rowmax", [128, 1])
        gmax = sb("gmax", [1, E])
        gspread = sb("gspread", [1, 128])
        mx = sb("mx", [128, 1])
        rowsum = sb("rowsum", [128, 1])
        zcol = sb("zcol", [128, 1])
        nmxb = sb("nmxb", [128, E])
        rzb = sb("rzb", [128, E])
        kth = sb("kth", [128, 1], i32)
        bit = sb("bit", [128, 1], i32)
        cand = sb("cand", [128, 1], i32)
        keep = sb("keep", [128, 1], i32)
        cnt = sb("cnt", [128, 1])
        nbelow = sb("nbelow", [128, 1])
        col = sb("col", [128, 3])
        identb = sb("identb", [128, 128], bf16)
        tile_no = sb("tile_no", [T, PX], bf16)
        hiT = sb("hiT", [T, E * TB], bf16)
        loT = sb("loT", [T, E * TB], bf16)
        hot_hi = sb("hot_hi", [T, HI, PX], bf16)
        hot_lo = sb("hot_lo", [T, 3 * LO, PX], bf16)
        found = sb("found", [HI, 2, 2, LO])
        ids = sb("ids", [HI, 2, LO], u32)
        idx_next = sb("idx_next", [128, 2, ST], u32)
        idx = sb("idx", [128, 2, ST], u32)
        w1s = [sb(f"w1s{j}", [128, FF]) for j in range(2)]
        w2s = [sb(f"w2s{j}", [128, FC, F]) for j in range(2)]
        b1s = [sb(f"b1s{j}", [128, FC]) for j in range(2)]
        b2s = [sb(f"b2s{j}", [128, F]) for j in range(2)]
        cur = sb("cur", [128, 3, 2])
        xs = [sb(f"xs{j}", [128, ST, F]) for j in range(2)]
        xsT = [sb(f"xsT{j}", [128, ST * 128]) for j in range(2)]
        val = sb("val", [128, 2, ST])
        hid = [sb(f"hid{i}", [128, HALF_T * 128]) for i in range(2 * FC)]
        y = [sb(f"y{i}", [128, HALF_T, F]) for i in range(2)]

        logits_in, consts_in = sem("logits_in"), sem("consts_in")
        rowmax_done, rowmax_ready, gmax_done, spread_done = map(sem, ("rowmax_done", "rowmax_ready", "gmax_done", "spread_done"))
        mx_ready, mx_done, dist_done, rowsum_done = map(sem, ("mx_ready", "mx_done", "dist_done", "rowsum_done"))
        z_ready, z_done, stats_ready, stats_done = map(sem, ("z_ready", "z_done", "stats_ready", "stats_done"))
        cand_done, cnt_done, total_ready, keep_done, kth_done, bit_done = map(
            sem, ("cand_done", "cnt_done", "total_ready", "keep_done", "kth_done", "bit_done"))
        pick_step, ties_ready, offset_ready, split_ready, splitT_done = map(
            sem, ("pick_step", "ties_ready", "offset_ready", "split_ready", "splitT_done"))
        hot_done, scaled_done, list_ready, found_done, ids_done, idx_in = map(
            sem, ("hot_done", "scaled_done", "list_ready", "found_done", "ids_done", "idx_in"))
        idx_done, cur_done, val_ready, exp_done, val_done = map(
            sem, ("idx_done", "cur_done", "val_ready", "exp_done", "val_done"))
        gathered = [sem(f"gathered{j}") for j in range(2)]
        weights_in = [sem(f"weights_in{j}") for j in range(2)]
        xsT_ready, xsT_done, hid_ready, hid_done, y_ready, y_done, yw_done, scattered = map(
            sem, ("xsT_ready", "xsT_done", "hid_ready", "hid_done", "y_ready", "ysum_done", "yw_done", "scattered"))

        def c(at, rows, cols):
            return cst[0:rows, at:at + cols]

        PER = 2 * 2

        with nc.Block() as block:

            @block.sync
            def _(sp):
                sp.dma_start(lgt[:, :], logits.rearrange("e b t -> (e b) t")).then_inc(logits_in, 16)

                def weights(k):
                    for j in range(2):
                        e = bass.ds(2 * k + j, 1)
                        used = sp.to_reg(sp.snap(PER * k + 2))
                        sp.wait_ge(y_ready, used)
                        sp.wait_ge(y_done, used)
                        sp.dma_start(w1s[j][:, :], w1[e, :, :].rearrange("e d f -> d (e f)")).then_inc(weights_in[j], 16)
                        sp.dma_start(w2s[j][:, :, :], w2[e, :, :].rearrange("e (c p) d -> p (e c) d", c=FC))\
                            .then_inc(weights_in[j], 16)
                        sp.dma_start(b1s[j][:, :], b1[:, e, :].rearrange("p e c -> p (e c)")).then_inc(weights_in[j], 16)
                        sp.dma_start(b2s[j][:, :], b2[bass.ds((2 * k + j) * F, F)].partition_broadcast(128))\
                            .then_inc(weights_in[j], 16)

                def indices(k):
                    listed, copied = sp.to_reg(sp.snap(k + 1)), sp.to_reg(sp.snap(k + 1))
                    sp.wait_ge(ids_done, listed)
                    sp.wait_ge(idx_done, copied)
                    for h in range(2):
                        sp.dma_start(idx_next[HI * h:HI * (h + 1), :, :], ids[:, :, ST * h:ST * (h + 1)])\
                            .then_inc(idx_in, 16)

                sp.sem_inc(idx_done, 1)
                indices(0)
                weights(0)
                with sp.Fori(0, PAIRS - 1) as k:
                    indices(k + 1)
                    weights(k + 1)

            @block.tensor
            def _(pe):
                pe.wait_ge(rowmax_done, 1)
                nc.tensor.transpose(banks[0][0:1, 0:128], rowmax[:, :], c(IDENT, 128, 128)).then_inc(rowmax_ready, 1)
                pe.wait_ge(spread_done, 1)
                nc.tensor.matmul(banks[1][:, 0:1], gspread[:, :], c(ONES, 1, 1), start=True, stop=True)\
                    .then_inc(mx_ready, 1)
                pe.wait_ge(rowsum_done, 1)
                nc.tensor.matmul(banks[2][:, 0:1], c(GROUP, 128, 128), rowsum[:, :], start=True, stop=True)\
                    .then_inc(z_ready, 1)
                pe.wait_ge(z_done, 1)
                nc.tensor.matmul(banks[3][:, 0:E], mx[:, 0:1].to_broadcast([128, 128]), c(PICK, 128, E),
                                 start=True, stop=True)
                nc.tensor.matmul(banks[3][:, E:2 * E], zcol[:, 0:1].to_broadcast([128, 128]), c(PICK, 128, E),
                                 start=True, stop=True).then_inc(stats_ready, 1)
                with pe.Fori(0, ROUNDS) as r:
                    pe.wait_ge(cnt_done, r + 1)
                    nc.tensor.matmul(banks[0][:, 0:1], c(GROUP, 128, 128), cnt[:, :], start=True, stop=True)\
                        .then_inc(total_ready, 1)
                pe.wait_ge(pick_step, 3)
                nc.tensor.matmul(banks[1][:, 0:1], c(GROUP, 128, 128), nbelow[:, :], start=True, stop=True)
                nc.tensor.matmul(banks[1][:, 1:2], c(EARLIER, 128, 128), work[:, L - 1:L], start=True, stop=True)\
                    .then_inc(ties_ready, 1)
                pe.wait_ge(pick_step, 9)
                nc.tensor.matmul(banks[2][:, 0:1], c(EARLIER, 128, 128), slot[:, L - 1:L], start=True, stop=True)\
                    .then_inc(offset_ready, 1)
                pe.wait_ge(pick_step, 16)
                for s, src in enumerate((hib, lob)):
                    for ch in range(CH):
                        m = nc.tensor.transpose(
                            banks[3 + 2 * s + ch // 4][0:T, :].bitcast(bf16)[:, (ch % 4) * 128:(ch % 4 + 1) * 128],
                            src[:, ch * T:(ch + 1) * T], identb[:, :])
                m.then_inc(split_ready, 1)

                def lists(k):
                    pe.wait_ge(hot_done, k + 1)
                    pe.wait_ge(scaled_done, 2 * k + 2)
                    for j in range(2):
                        for t in range(TB):
                            at = j * TB + t
                            m = nc.tensor.matmul(banks[6][0:HI, 2 * LO * j:2 * LO * (j + 1)], hot_hi[:, :, at],
                                                 hot_lo[:, LO:3 * LO, at], start=(t == 0), stop=(t == TB - 1))
                    m.then_inc(list_ready, 1)

                def turn(k):
                    for j in range(2):
                        pe.wait_ge(gathered[j], 16 * ST * k + 16 * ST)
                        for h in range(2):
                            pe.wait_ge(xsT_done, PER * k + 2 * j + h + 1)
                            for g in range(HALF_T):
                                m = nc.tensor.transpose(banks[h][:, g * 128:(g + 1) * 128],
                                                        xs[j][:, HALF_T * h + g, :], c(IDENT, 128, 128))
                            m.then_inc(xsT_ready, 1)
                    pe.wait_ge(cur_done, k + 1)
                    pe.wait_ge(xsT_done, PER * k + 6)
                    for j in range(2):
                        for g in range(ST):
                            m = nc.tensor.matmul(banks[7][:, ST * j + g:ST * j + g + 1],
                                                 xsT[j][:, g * 128:(g + 1) * 128], cur[:, 2, j:j + 1],
                                                 start=True, stop=True)
                    m.then_inc(val_ready, 1)

                def expert(k, j):
                    pe.wait_ge(weights_in[j], 64 * k + 64)
                    for h in range(2):
                        for f in range(FC):
                            pe.wait_ge(hid_done, (2 * k + j) * 2 * FC + h * FC + f + 1)
                            nc.tensor.matmul(banks[2 + f % 2][:, :], w1s[j][:, f * 128:(f + 1) * 128],
                                             xsT[j][:, h * 512:(h + 1) * 512], start=True, stop=True)\
                                .then_inc(hid_ready, 1)
                    for h in range(2):
                        pe.wait_ge(hid_done, (2 * k + j) * 2 * FC + (h + 1) * FC + 2)
                        pe.wait_ge(y_done, (2 * k + j) * 2 + h + 1)
                        for g in range(HALF_T):
                            for f in range(FC):
                                m = nc.tensor.matmul(banks[4 + h][:, g * 128:(g + 1) * 128],
                                                     hid[h * FC + f][:, g * 128:(g + 1) * 128], w2s[j][:, f, :],
                                                     start=(f == 0), stop=(f == FC - 1))
                        m.then_inc(y_ready, 1)

                pe.sem_inc(y_ready, 2)
                pe.sem_inc(list_ready, 1)
                pe.wait_ge(splitT_done, 1)
                lists(0)
                with pe.Fori(0, PAIRS - 1) as k:
                    turn(k)
                    expert(k, 0)
                    lists(k + 1)
                    expert(k, 1)
                turn(PAIRS - 1)
                expert(PAIRS - 1, 0)
                expert(PAIRS - 1, 1)

            @block.scalar
            def _(sc):
                sc.wait_ge(dist_done, 1)
                nc.scalar.activation(work[:, :], dist[:, :], ACT.Exp, scale=-1.0, accum_out=rowsum[:, :])\
                    .then_inc(rowsum_done, 1)

                def values(k):
                    sc.wait_ge(val_ready, k + 1)
                    sc.wait_ge(val_done, k + 1)
                    sc.wait_ge(yw_done, PER * k + 1)
                    for j in range(2):
                        m = nc.scalar.activation(val[:, j, :], banks[7][:, ST * j:ST * (j + 1)], ACT.Exp,
                                                 bias=cur[:, 0, j:j + 1])
                    m.then_inc(exp_done, 1)

                def expert(k, j):
                    for h in range(2):
                        for f in range(FC):
                            sc.wait_ge(hid_ready, (2 * k + j) * 2 * FC + h * FC + f + 1)
                            if f == 0:
                                sc.wait_ge(y_ready, (2 * k + j) * 2 + h + 1)
                            nc.scalar.activation(hid[h * FC + f][:, :], banks[2 + f % 2][:, :], ACT.Gelu,
                                                 bias=b1s[j][:, f:f + 1]).then_inc(hid_done, 1)

                sc.sem_inc(hid_done, 2)
                with sc.Fori(0, PAIRS) as k:
                    values(k)
                    for j in range(2):
                        expert(k, j)

            @block.vector
            def _(ve):
                ve.wait_ge(logits_in, 16)
                nc.vector.tensor_copy(identb[:, :], c(IDENT, 128, 128))
                nc.vector.tensor_copy(tile_no[:, :], c(TILE_NO, T, PX))
                nc.vector.memset(scan_one[:, :], 1.0)
                nc.vector.memset(kth[:, :], 0).then_inc(kth_done, 1)
                nc.vector.memset(bit[:, :], 1 << (ROUNDS - 1)).then_inc(bit_done, 1)
                nc.vector.reduce_max(rowmax[:, :], lgt[:, :], X).then_inc(rowmax_done, 1)
                ve.wait_ge(rowmax_ready, 1)
                nc.vector.reduce_max(gmax[:, :], banks[0][0:1, 0:128].rearrange("p (e b) -> p e b", e=E), X)\
                    .then_inc(gmax_done, 1)
                ve.wait_ge(gmax_done, 1)
                nc.vector.tensor_copy(gspread[:, :].rearrange("p (e b) -> p e b", e=E),
                                      gmax[:, :].unsqueeze(2).to_broadcast([1, E, B])).then_inc(spread_done, 1)
                ve.wait_ge(mx_ready, 1)
                nc.vector.tensor_copy(mx[:, :], banks[1][:, 0:1]).then_inc(mx_done, 1)
                ve.wait_ge(mx_done, 1)
                nc.vector.tensor_scalar(dist[:, :], lgt[:, :], -1.0, mx[:, 0:1], ALU.mult, ALU.add)\
                    .then_inc(dist_done, 1)
                ve.wait_ge(z_ready, 1)
                nc.vector.tensor_copy(zcol[:, :], banks[2][:, 0:1]).then_inc(z_done, 1)
                ve.wait_ge(stats_ready, 1)
                nc.vector.tensor_scalar(nmxb[:, :], banks[3][:, 0:E], -1.0, None, ALU.mult)
                nc.vector.reciprocal(rzb[:, :], banks[3][:, E:2 * E]).then_inc(stats_done, 1)
                ve.wait_ge(dist_done, 1)
                with ve.Fori(0, ROUNDS) as r:
                    ve.wait_ge(kth_done, r + 1)
                    ve.wait_ge(bit_done, r + 1)
                    nc.vector.tensor_tensor(cand[:, :], kth[:, :], bit[:, :], ALU.bitwise_or).then_inc(cand_done, 1)
                    ve.wait_ge(cand_done, r + 1)
                    nc.vector.tensor_scalar(below[:, :], dist[:, :], cand[:, :].bitcast(f32), None, ALU.is_lt,
                                            ALU.add, accum_out=cnt[:, :]).then_inc(cnt_done, 1)
                    ve.wait_ge(cand_done, r + 1)
                    nc.vector.tensor_scalar(bit[:, :], bit[:, :], 1, None, ALU.logical_shift_right)\
                        .then_inc(bit_done, 1)
                    ve.wait_ge(total_ready, r + 1)
                    nc.vector.tensor_scalar(keep[:, :], banks[0][:, 0:1], float(CAP), None, ALU.is_lt)\
                        .then_inc(keep_done, 1)
                    kept = ve.to_reg(ve.snap(r + 1))
                    ve.wait_ge(logits_in, 16)
                    ve.wait_ge(keep_done, kept)
                    nc.vector.copy_predicated(kth[:, :], keep[:, :], cand[:, :]).then_inc(kth_done, 1)

                step = [0]

                def then(ins):
                    step[0] += 1
                    ins.then_inc(pick_step, 1)
                    ve.wait_ge(pick_step, step[0])

                ve.wait_ge(kth_done, ROUNDS + 1)
                edge = kth[:, :].bitcast(f32)
                then(nc.vector.tensor_scalar(below[:, :], dist[:, :], edge, None, ALU.is_lt, ALU.add,
                                             accum_out=nbelow[:, :]))
                then(nc.vector.tensor_scalar(ties[:, :], dist[:, :], edge, None, ALU.is_equal))
                then(nc.vector.tensor_tensor_scan(work[:, :], scan_one[:, :], ties[:, :], 0.0, ALU.mult, ALU.add))
                ve.wait_ge(ties_ready, 1)
                then(nc.vector.tensor_copy(col[:, 0:2], banks[1][:, 0:2]))
                then(nc.vector.tensor_tensor(col[:, 2:3], col[:, 0:1], col[:, 1:2], ALU.add))
                then(nc.vector.tensor_scalar(col[:, 2:3], col[:, 2:3], -1.0, float(CAP), ALU.mult, ALU.add))
                then(nc.vector.scalar_tensor_tensor(chosen[:, :], work[:, :], col[:, 2:3], ties[:, :],
                                                    ALU.is_le, ALU.mult))
                then(nc.vector.tensor_tensor(chosen[:, :], chosen[:, :], below[:, :], ALU.add))
                then(nc.vector.tensor_tensor_scan(slot[:, :], scan_one[:, :], chosen[:, :], 0.0, ALU.mult, ALU.add))
                ve.wait_ge(offset_ready, 1)
                then(nc.vector.tensor_copy(col[:, 0:1], banks[2][:, 0:1]))
                then(nc.vector.scalar_tensor_tensor(work[:, :], slot[:, :], col[:, 0:1], chosen[:, :],
                                                    ALU.add, ALU.mult))
                then(nc.vector.tensor_scalar(sloti[:, :], work[:, :], -1.0, None, ALU.add))
                then(nc.vector.tensor_scalar(hii[:, :], sloti[:, :], LO.bit_length() - 1, None,
                                             ALU.arith_shift_right))
                then(nc.vector.tensor_scalar(loi[:, :], sloti[:, :], LO - 1, None, ALU.bitwise_and))
                then(nc.vector.tensor_copy(hib[:, :], hii[:, :]))
                then(nc.vector.tensor_copy(lob[:, :], loi[:, :]))
                ve.wait_ge(split_ready, 1)
                for s, dst in enumerate((hiT, loT)):
                    for ch in range(CH):
                        src = banks[3 + 2 * s + ch // 4][0:T, :].bitcast(bf16)[:, (ch % 4) * 128:(ch % 4 + 1) * 128]
                        m = nc.vector.tensor_copy(
                            dst[:, :].rearrange("p (e c b) -> p e c b", e=E, c=CH)[:, :, ch, :],
                            src.rearrange("p (e b) -> p e b", e=E))
                m.then_inc(splitT_done, 1)

                def one_hots(k):
                    here = bass.ds(k * PX, PX) if not isinstance(k, int) else slice(k * PX, (k + 1) * PX)
                    ve.wait_ge(list_ready, k + 1)
                    for r in range(HI):
                        nc.vector.tensor_scalar(hot_hi[:, r, :], hiT[:, here], float(r), None, ALU.is_equal)
                    for r in range(LO):
                        m = nc.vector.tensor_scalar(hot_lo[:, r, :], loT[:, here], float(r), None, ALU.is_equal)
                    m.then_inc(hot_done, 1)
                    ve.wait_ge(hot_done, k + 1)
                    nc.vector.tensor_scalar(hot_lo[:, LO:2 * LO, :], hot_lo[:, 0:LO, :], c(ROW, T, 1), None,
                                            ALU.mult).then_inc(scaled_done, 1)
                    nc.vector.tensor_tensor(hot_lo[:, 2 * LO:3 * LO, :], hot_lo[:, 0:LO, :],
                                            tile_no[:, :].unsqueeze(1).to_broadcast([T, LO, PX]),
                                            ALU.mult).then_inc(scaled_done, 1)

                def tokens(k):
                    listed = ve.to_reg(ve.snap(k + 2)) if not isinstance(k, int) else k + 2
                    sent = ve.to_reg(ve.snap(32 * k + 32)) if not isinstance(k, int) else 32 * k + 32
                    ve.wait_ge(logits_in, 16)
                    ve.wait_ge(list_ready, listed)
                    nc.vector.tensor_copy(found[:, :, :, :].rearrange("p a b c -> p (a b c)"),
                                          banks[6][0:HI, 0:4 * LO]).then_inc(found_done, 1)
                    ve.wait_ge(found_done, k + 1)
                    ve.wait_ge(idx_in, sent)
                    nc.vector.scalar_tensor_tensor(ids[:, :, :], found[:, :, 1, :], float(T), found[:, :, 0, :],
                                                   ALU.mult, ALU.add).then_inc(ids_done, 1)

                def turn(k):
                    two = bass.ds(2 * k, 2) if not isinstance(k, int) else slice(2 * k, 2 * k + 2)
                    arrived = ve.to_reg(ve.snap(32 * k + 64)) if not isinstance(k, int) else 32 * k + 64
                    past = ve.to_reg(ve.snap(32 * ST * k)) if not isinstance(k, int) else 32 * ST * k
                    done = ve.to_reg(ve.snap(PER * k + 2)) if not isinstance(k, int) else PER * k + 2
                    ve.wait_ge(logits_in, 16)
                    ve.wait_ge(idx_in, arrived)
                    if not isinstance(past, int) or past > 0:
                        ve.wait_ge(scattered, past)
                    ve.wait_ge(y_ready, done)
                    nc.vector.tensor_copy(idx[:, :, :], idx_next[:, :, :]).then_inc(idx_done, 1)
                    for i, src in enumerate((nmxb, rzb, wr_sb)):
                        m = nc.vector.tensor_scalar(cur[:, i, :], src[:, two], 1.0, None, ALU.mult)
                    m.then_inc(cur_done, 1)
                    for j in range(2):
                        for h in range(2):
                            ready = (ve.to_reg(ve.snap(PER * k + 2 * j + h + 2)) if not isinstance(k, int)
                                     else PER * k + 2 * j + h + 2)
                            ve.wait_ge(logits_in, 16)
                            ve.wait_ge(xsT_ready, ready)
                            nc.vector.tensor_copy(xsT[j][:, h * 512:(h + 1) * 512], banks[h][:, :])\
                                .then_inc(xsT_done, 1)
                    ve.wait_ge(exp_done, k + 1)
                    nc.vector.tensor_tensor(val[:, :, :], val[:, :, :],
                                            cur[:, 1, :].unsqueeze(2).to_broadcast([128, 2, ST]), ALU.mult)\
                        .then_inc(val_done, 1)

                def expert(k, j):
                    for h in range(2):
                        ve.wait_ge(y_ready, (2 * k + j) * 2 + h + 3)
                        past = (2 * k + j) * 16 * ST
                        if not isinstance(past, int) or past > 0:
                            ve.wait_ge(scattered, past)
                        nc.vector.tensor_tensor(y[h][:, :, :], banks[4 + h][:, :].rearrange("p (g d) -> p g d", g=HALF_T),
                                                b2s[j][:, :].unsqueeze(1).to_broadcast([128, HALF_T, F]), ALU.add)\
                            .then_inc(y_done, 1)

                ve.sem_inc(xsT_done, 2)
                ve.sem_inc(val_done, 1)
                ve.sem_inc(y_done, 2)
                ve.wait_ge(splitT_done, 1)
                one_hots(0)
                tokens(0)

                def pair(k):
                    turn(k)
                    one_hots(k + 1)
                    expert(k, 0)
                    tokens(k + 1)
                    expert(k, 1)

                pair(0)
                with ve.Fori(1, PAIRS - 1) as k:
                    pair(k)
                turn(PAIRS - 1)
                expert(PAIRS - 1, 0)
                expert(PAIRS - 1, 1)

            @block.gpsimd
            def _(po):
                rows = out.rearrange("b t f -> (b t) f")

                def reg(k, value):
                    return value if isinstance(k, int) else po.to_reg(po.snap(value))

                def gather(k):
                    for j in range(2):
                        listed, turned = reg(k, 32 * k + 64), reg(k, PER * k + 1)
                        po.wait_ge(logits_in, 16)
                        po.wait_ge(idx_in, listed)
                        po.wait_ge(xsT_ready, turned)
                        for g in range(ST):
                            nc.gpsimd.indirect_dma_start(
                                xs[j][:, g, :], None, x2_rows,
                                bass.IndirectOffsetOnAxis(idx_next[:, j, g:g + 1], 0)).then_inc(gathered[j], 16)

                def expert(k, j):
                    for h in range(2):
                        po.wait_ge(val_done, k + 2)
                        po.wait_ge(y_done, (2 * k + j) * 2 + h + 3)
                        nc.gpsimd.tensor_tensor(
                            y[h][:, :, :], y[h][:, :, :],
                            val[:, j, HALF_T * h:HALF_T * (h + 1)].unsqueeze(2).to_broadcast([128, HALF_T, F]),
                            ALU.mult).then_inc(yw_done, 1)
                    for h in range(2):
                        weighted = reg(k, (2 * k + j) * 2 + h + 2)
                        added = reg(k, (2 * k + j) * 16 * ST)
                        po.wait_ge(logits_in, 16)
                        po.wait_ge(yw_done, weighted)
                        if h == 0 and (not isinstance(added, int) or added > 0):
                            po.wait_ge(scattered, added)
                        for g in range(HALF_T):
                            nc.gpsimd.indirect_dma_start(
                                rows, bass.IndirectOffsetOnAxis(idx[:, j, HALF_T * h + g:HALF_T * h + g + 1], 0),
                                y[h][:, g, :], None, compute_op=ALU.add).then_inc(scattered, 16)

                po.sem_inc(yw_done, 1)
                po.sem_inc(idx_in, 32)
                po.sem_inc(xsT_ready, 1)
                gather(0)

                def pair(k):
                    expert(k, 0)
                    gather(k + 1)
                    expert(k, 1)

                pair(0)
                with po.Fori(1, PAIRS - 1) as k:
                    pair(k)
                expert(PAIRS - 1, 0)
                expert(PAIRS - 1, 1)
                po.wait_ge(scattered, 16 * ST * E)


def kernel(**inputs):
    import concourse.bacc as _bacc
    from concourse import mybir as _mybir
    from concourse.bass_utils import run_bass_kernel_spmd as _run

    a = {k: np.asarray(v) for k, v in inputs.items()}

    def col(name):
        return a[name].reshape(-1, 128).T

    vecs = np.concatenate(
        [col("L0_tok_bias")] + [col("L0_attn_b" + s) for s in "qkvg"]
        + [a["L0_attn_cw" + s][:, 0, :] for s in "qkv"] + [col("L0_attn_cb" + s) for s in "qkv"]
        + [col("L0_attn_norm_w"), col("L0_attn_bo")], axis=1)
    arrays = {
        "in_x": a["x"], "in_consts": constants(), "in_vecs": vecs,
        "in_wconv": a["L0_tok_kernel"].reshape(TAPS * CIN, F),
        "in_wlin": np.stack([a["L0_attn_W" + s].T for s in "qkvgo"]),
        "in_wab": np.concatenate([a["L0_attn_Wa"].T, a["L0_attn_Wb"].T], axis=1),
        "in_bab": np.concatenate([a["L0_attn_ba"], a["L0_attn_bb"]]),
        "in_wr": a["L0_ffn_Wr"], "in_w1": a["L0_ffn_W1"],
        "in_b1": a["L0_ffn_b1"].reshape(E, FF // 128, 128).transpose(2, 0, 1),
        "in_w2": a["L0_ffn_W2"], "in_b2": a["L0_ffn_b2"].reshape(E * 128),
    }
    arrays = {k: np.ascontiguousarray(v) for k, v in arrays.items()}
    nc = _bacc.Bacc("TRN2", target_bir_lowering=False, num_devices=1)
    args = [nc.dram_tensor(k, v.shape, _mybir.dt.from_np(v.dtype), kind="ExternalInput").ap()
            for k, v in arrays.items()]
    out = nc.dram_tensor("out_0", (B, L, F), _mybir.dt.float32, kind="ExternalOutput").ap()
    x2_rows = nc.dram_tensor("x2_rows", (N, F), _mybir.dt.float32, kind="Internal").ap()
    logits = nc.dram_tensor("logits", (E, B, L), _mybir.dt.float32, kind="Internal").ap()
    tower(nc, *args, out, x2_rows, logits)
    r = _run(nc, [arrays], core_ids=[0])
    return r.results[0]["out_0"]
```

```python
from contextlib import ExitStack

import numpy as np
import concourse.bass as bass
from concourse import mybir
from concourse.alu_op_type import AluOpType as ALU

B, LX, CIN = 16, 750, 64
TAPS, F = 9, 128
L = LX - TAPS + 1
T = 106
CH = L // T
XR = T + TAPS - 2
XS = XR + 1
Q = 4
W = Q * T
OCT = B // (2 * Q)
E, FF, CAP = 8, 512, 1024
N = B * L
ST = CAP // 128
DW = 4
HALO = DW - 1
LEVELS = 7
HW = 64
TILES = N // T
HI, LO = 64, 16
assert CH * T == L and HI * LO == CAP and B * E == 128

IDENT, TRI_LE, TRI_GT, BAND = 0, 128, 128 + T, 128 + 2 * T
CENTRE = BAND + T
MEAN, ONES, GROUP, EARLIER, PICK = CENTRE + 128, CENTRE + 256, CENTRE + 384, CENTRE + 512, CENTRE + 640
MASKS = PICK + E
TILE_NO = MASKS + 2 * LEVELS * Q * HW
SMALL = TILE_NO + 2 * B * CH
HALF, EPS, TINY, LNS, ONE, ROW, TINYSQ = range(SMALL, SMALL + 7)
NCONST = SMALL + 8
V_TOKB, V_BQ, V_BK, V_BV, V_BG, V_CW, V_CB, V_NORM, V_BO = 0, 1, 2, 3, 4, 5, 17, 20, 21
NVEC = 22
LN_SCALE = 2.0 ** 30
SILU_SET, LOG_SET = "silu_and_others", "natural_log_exp_and_others"
LAM = 1.0 / (1.0 + 1e-7)


def constants():
    c = np.zeros((128, NCONST), np.float32)
    i, j = np.indices((128, 128))
    c[:, IDENT:IDENT + 128] = i == j
    c[:T, TRI_LE:TRI_LE + T] = (i <= j)[:T, :T]
    c[:T, TRI_GT:TRI_GT + T] = (i > j)[:T, :T]
    c[:, BAND:BAND + T] = ((i >= j) & (i < j + TAPS))[:, :T]
    c[:, CENTRE:CENTRE + 128] = (i == j) - 1.0 / F
    c[:, MEAN:MEAN + 128] = 1.0 / F
    c[:, ONES:ONES + 128] = 1.0
    c[:, GROUP:GROUP + 128] = i // B == j // B
    c[:, EARLIER:EARLIER + 128] = (i // B == j // B) & (i < j)
    c[:, PICK:PICK + E] = (i == B * j)[:, :E]
    for m in range(LEVELS):
        s = 1 << m
        low = (i // (2 * s) == j // (2 * s)) & (i // s > j // s)
        even, odd = (j[0] // s) % 2 == 0, (j[0] // s) % 2 == 1
        at = MASKS + 2 * m * Q * HW
        c[:, at:at + Q * HW] = np.tile(low[:, even], Q)
        c[:, at + Q * HW:at + 2 * Q * HW] = np.tile(low.T[:, odd], Q)
    c[:, TILE_NO:SMALL] = np.tile(np.add.outer(np.arange(CH), CH * np.arange(B)).ravel(), 2)
    c[:, HALF] = 0.5
    c[:, EPS] = 1e-5
    c[:, TINY] = 2.0 ** -62
    c[:, LNS] = 0.5 * np.log(LN_SCALE)
    c[:, ONE] = 1.0
    c[:, ROW] = np.arange(128)
    return c


def tower(nc, x, consts, vecs, wconv, wlin, wab, bab, wr, w1, b1, w2, b2, out, x2_rows, logits):
    f32, bf16, i32, u32 = mybir.dt.float32, mybir.dt.bfloat16, mybir.dt.int32, mybir.dt.uint32
    ACT = mybir.ActivationFunctionType
    X = mybir.AxisListType.X
    ctx = ExitStack()
    with ctx:
        banks = [ctx.enter_context(nc.psum_tensor(f"bank{i}", [128, 512], f32)) for i in range(8)]
        cst = ctx.enter_context(nc.sbuf_tensor("cst", [128, NCONST], f32))
        wr_sb = ctx.enter_context(nc.sbuf_tensor("wr_sb", [128, E], f32))
        tokens_phase(nc, banks, cst, wr_sb, x, consts, vecs, wconv, wlin, wab, bab, wr, out, x2_rows,
                     logits, f32, i32, ACT, X)
        experts_phase(nc, banks, cst, wr_sb, w1, b1, w2, b2, out, x2_rows, logits,
                      f32, bf16, i32, u32, ACT, X)


def tokens_phase(nc, banks, cst, wr_sb, x, consts, vecs, wconv, wlin, wab, bab, wr, out, x2_rows,
                 logits, f32, i32, ACT, X):
    ctx = ExitStack()
    with ctx:
        def sb(name, shape, dt=f32):
            return ctx.enter_context(nc.sbuf_tensor(name, shape, dt))

        def pair(name, shape):
            return [sb(f"{name}{q}", shape) for q in range(2)]

        def sem(name):
            return ctx.enter_context(nc.semaphore(name))

        def sems(name):
            return [sem(f"{name}{q}") for q in range(2)]

        vec = sb("vec", [128, NVEC])
        conv_w = sb("conv_w", [128, 5, F])
        lin_w = sb("lin_w", [128, 5, 128])
        ab_w = sb("ab_w", [128, 2])
        ab_b = sb("ab_b", [128, 2])
        xin = pair("xin", [XS, Q, 2 * CIN])
        xsq = pair("xsq", [XS, Q, CIN])
        ssq = pair("ssq", [XS, Q])
        xT = pair("xT", [128, Q, XR])
        wcol = pair("wcol", [T, Q])
        scl = pair("scl", [128, W])
        hT = pair("hT", [128, W])
        sqr = pair("sqr", [128, W])
        rstd = pair("rstd", [128, W])
        xn = pair("xn", [128, W])
        hres = pair("hres", [128, W])
        sqt = pair("sqt", [128, W])
        rst = pair("rst", [128, W])
        xt = pair("xt", [128, W])
        gn = pair("gn", [128, W])
        lin = [pair(f"lin{j}", [128, Q, T + HALO]) for j in range(3)]
        gate = pair("gate", [128, W])
        act = [pair(f"act{j}", [128, W]) for j in range(3)]
        zab = pair("zab", [T, Q, 2])
        nab = pair("nab", [T, Q, 2])
        eab = pair("eab", [T, Q, 2])
        gab = pair("gab", [T, Q, 2])
        beta = pair("beta", [T, Q])
        nbeta = pair("nbeta", [T, Q])
        sq2 = pair("sq2", [128, W])
        rq = pair("rq", [128, W])
        kg = pair("kg", [128, W])
        qg = pair("qg", [128, W])
        gl = pair("gl", [T, W])
        dec = pair("dec", [T, W])
        eg = pair("eg", [128, W])
        eb = pair("eb", [T, W])
        ua = pair("ua", [T, Q * 128])
        pt = pair("pt", [T, W])
        inv = pair("inv", [T, Q * 128])
        invT = pair("invT", [T, Q * 128])
        ps = pair("ps", [T, Q * 128])
        rhs = pair("rhs", [T, Q * 128])
        u = pair("u", [T, Q * 128])
        ue = pair("ue", [T, Q * 128])
        kN = pair("kN", [T, Q * 128])
        st = pair("st", [128, Q * 128])
        h2N = pair("h2N", [T, Q * 128])
        x2N = pair("x2N", [T, Q * 128])
        lg = pair("lg", [E, W])

        S, PLACE = {}, {}
        for names in ("xin_loaded", "xsq_done", "ssq_done", "xT_ready wsum_ready conv_ready scale_ready",
                      "xT_done scale_done tanh_done", "wmax_done wroot_done weps_done wrec_done wcol_done",
                      "v_done h_done xn_done", "ovar_ready h2m_ready h2var_ready",
                      "xmsq_done", "osq_done h2sq_done", "res_done", "lnv_done rstd_done",
                      "lnk_done rk_done", "lno_done rstdo_done lnh2_done rstdh2_done",
                      "xm_ready var_ready linq_ready link_ready linv_ready gate_ready", "linq_done link_done linv_done",
                      "zab_done gatelin_done", "halo_done", "tap0_done", "tap_done",
                      "z_done nz_done az_done mab_done g_done", "eab_done lab_done beta_done", "silu_done",
                      "sqqk_done", "lnq_done rq_done", "qn_done kn_done kg_done ua_done pt_done",
                      "gl_done", "edec_done eg_done", "dec_done nbeta_done eb_done",
                      "qg_done", "D_ready cum_ready nq_ready nk_ready kk_ready kq_ready kN_ready R_ready",
                      "kN_done rhs_done", "eye_done", "P_ready", "P_done", "XY_ready", "inv_done",
                      "invT_done", "W_ready O_ready dS_ready", "u_done", "ue_done",
                      "decay_st_done", "st_done", "on_done gated_done h2_done x2_done",
                      "y_ready lg_ready x2N_ready h2N_ready", "lg_done h2N_done", "x2N_done",
                      "lg_stored", "h2_stored", "x2_stored"):
            order = names.split()
            shared = sems(order[0] if len(order) == 1 else f"{order[0]}_to_{order[-1]}")
            for k, name in enumerate(order):
                S[name], PLACE[name] = shared, (len(order), k + 1)

        AHEAD = {"xsq_done": 1, "ssq_done": 1, "scale_ready": 1, "h2N_done": 1, "x2N_done": 1,
                 "tap_done": 1, "rhs_done": 1, "res_done": 1, "h2N_ready": 1, "halo_done": 1, "lg_stored": 16, "h2_stored": 16,
                 "x2_stored": 16}
        ahead = {id(S[name]): by for name, by in AHEAD.items()}

        def count(name, turn):
            per, at = PLACE[name]
            return turn * per - (per - at) + ahead.get(id(S[name]), 0)

        def give_ahead(eng, *names):
            for name in names:
                for q in range(2):
                    eng.sem_inc(S[name][q], AHEAD[name])

        weights_loaded = sem("weights_loaded")
        masks_loaded = sem("masks_loaded")
        cleared = sem("cleared")

        def bank(q, i):
            return banks[4 * q + i]

        def over(ap, width=T):
            return ap.unsqueeze(1).to_broadcast([ap.shape[0], Q, width])

        def along(ap, width):
            return ap.unsqueeze(2).to_broadcast([ap.shape[0], Q, width])

        def tiles(buf, width=T):
            return buf[:, :].rearrange("p (i t) -> p i t", i=Q) if width == T else \
                buf[:, :].rearrange("p (i d) -> p i d", i=Q)

        def c(at, rows, cols):
            return cst[0:rows, at:at + cols]

        def blocks(cols, lev, odd):
            s = 1 << lev
            return cols.rearrange("p (b s) -> p b s", s=2 * s)[:, :, s * odd:s * odd + s]

        def v(at):
            return vec[:, at:at + 1]

        NW = 9
        x_t = x.rearrange("b t c -> t b c")
        out_t = out.rearrange("b t f -> t b f")
        x2_t = x2_rows.rearrange("(b t) f -> t b f", b=B)

        with nc.Block() as block:

            @block.sync
            def _(sp):
                for part in (slice(0, MASKS), slice(TILE_NO, NCONST)):
                    sp.dma_start(cst[:, part], consts[:, part]).then_inc(weights_loaded, 16)
                sp.dma_start(vec[:, :], vecs).then_inc(weights_loaded, 16)
                sp.dma_start(conv_w[:, 0:4, :], wconv[0:512, :].rearrange("(k p) f -> p k f", k=4))\
                    .then_inc(weights_loaded, 16)
                sp.dma_start(conv_w[64:128, 4, :], wconv[512:576, :]).then_inc(weights_loaded, 16)
                sp.dma_start(lin_w[:, :, :], wlin.rearrange("k p f -> p k f")).then_inc(weights_loaded, 16)
                sp.dma_start(ab_w[:, :], wab).then_inc(weights_loaded, 16)
                sp.dma_start(ab_b[:, :], bab.partition_broadcast(128)).then_inc(weights_loaded, 16)
                sp.dma_start(wr_sb[:, :], wr).then_inc(weights_loaded, 16)
                give_ahead(sp, "lg_stored", "h2_stored", "x2_stored")
                def reg(value):
                    return value if isinstance(value, int) else sp.to_reg(sp.snap(value))

                def seqs(o, q):
                    first = o * (2 * Q) + q * Q
                    return bass.ds(first if isinstance(first, int) else sp.snap(first), Q)

                def load(n, o, ch):
                    for q in range(2):
                        rows = [x_t[bass.ds(ch * T + s, XS - s), seqs(o, q), :] for s in range(2)]
                        squared = reg(count("xsq_done", n))
                        transposed = reg(count("scale_ready", n))
                        sp.wait_ge(S["xsq_done"][q], squared)
                        sp.wait_ge(S["scale_ready"][q], transposed)
                        for s in range(2):
                            sp.dma_start(xin[q][0:XS - s, :, s * CIN:(s + 1) * CIN], rows[s])\
                                .then_inc(S["xin_loaded"][q], 16)

                def store(n, o, ch):
                    for q in range(2):
                        here = (bass.ds(ch * T, T), seqs(o, q))
                        sp.wait_ge(S["lg_done"][q], count("lg_done", n + 1))
                        sp.dma_start(logits[:, here[1], here[0]],
                                     lg[q][:, :].rearrange("e (i t) -> e i t", i=Q)).then_inc(S["lg_stored"][q], 16)
                        sp.wait_ge(S["x2N_done"][q], count("x2N_done", n + 1))
                        sp.dma_start(x2_t[here[0], here[1], :], tiles(x2N[q], 128)).then_inc(S["x2_stored"][q], 16)
                        sp.wait_ge(S["h2N_done"][q], count("h2N_done", n + 1))
                        sp.dma_start(out_t[here[0], here[1], :], tiles(h2N[q], 128)).then_inc(S["h2_stored"][q], 16)

                def stream(o):
                    with sp.Fori(0, CH - 2) as ch:
                        n = sp.snap(o * CH + ch)
                        load(n + 2, o, ch + 2)
                        store(n, o, ch)

                load(0, 0, 0)
                sp.dma_start(cst[:, MASKS:TILE_NO], consts[:, MASKS:TILE_NO]).then_inc(masks_loaded, 16)
                load(1, 0, 1)
                with sp.Fori(0, OCT - 1) as o:
                    stream(o)
                    for ch in range(2):
                        load((o + 1) * CH + ch, o + 1, ch)
                        store(o * CH + (CH - 2 + ch), o, CH - 2 + ch)
                stream(OCT - 1)
                for ch in range(2):
                    store((OCT - 1) * CH + CH - 2 + ch, OCT - 1, CH - 2 + ch)
                for q in range(2):
                    for k in ("lg_stored", "h2_stored", "x2_stored"):
                        sp.wait_ge(S[k][q], 16 * OCT * CH + 16)

            @block.tensor
            def _(pe):
                def wait(name, q, n):
                    pe.wait_ge(S[name][q], count(name, n + 1))

                def wait_last(name, q, n):
                    pe.wait_ge(S[name][q], count(name, n))

                def bmm(dst, lhs, rhs_, sem_, q):
                    for i in range(Q):
                        m = nc.tensor.matmul(dst(i), lhs(i), rhs_(i), start=True, stop=True)
                    m.then_inc(S[sem_][q], 1)

                def t(buf, q, i):
                    return buf[q][:, i * T:(i + 1) * T]

                def d(buf, q, i):
                    return buf[q][:, i * 128:(i + 1) * 128]

                def pT(q, b, i, rows=T):
                    return bank(q, b)[0:rows, i * T:(i + 1) * T]

                def half(q, b, i, at=0):
                    return bank(q, b)[0:T, at + i * HW:at + (i + 1) * HW]

                def pD(q, b, i, rows=T):
                    return bank(q, b)[0:rows, i * 128:(i + 1) * 128]

                def turn_x(n):
                    for q in range(2):
                        pe.wait_ge(S["xin_loaded"][q], 32 * n + 32)
                        wait_last("rhs_done", q, n)
                        for i in range(Q):
                            m = nc.tensor.transpose(bank(q, 0)[:, i * XR:(i + 1) * XR], xin[q][0:XR, i, :],
                                                    c(IDENT, XR, XR))
                        m.then_inc(S["xT_ready"][q], 1)

                def convolve(n):
                    for q in range(2):
                        wait("ssq_done", q, n)
                        nc.tensor.matmul(bank(q, 1)[0:T, 0:Q], c(BAND, XS, T), ssq[q][:, :],
                                         start=True, stop=True).then_inc(S["wsum_ready"][q], 1)
                        wait("xT_done", q, n)
                        for k in range(5):
                            p0 = 64 if k == 4 else 0
                            at = 2 * k if k < 4 else TAPS - 2
                            m = nc.tensor.matmul(bank(q, 0)[:, 0:W], conv_w[p0:128, k, :],
                                                 xT[q][p0:128, :, at:at + T],
                                                 start=(k == 0), stop=(k == 4))
                        m.then_inc(S["conv_ready"][q], 1)

                def spread_scale(n):
                    for q in range(2):
                        wait("wcol_done", q, n)
                        bmm(lambda i: pT(q, 1, i, 128),
                            lambda i: wcol[q][:, i:i + 1].to_broadcast([T, 128]),
                            lambda i: c(IDENT, T, T), "scale_ready", q)

                def centre(n, src, b, done, ready):
                    for q in range(2):
                        wait(done, q, n)
                        nc.tensor.matmul(bank(q, b)[:, 0:W], c(CENTRE, 128, 128), src[q][:, :],
                                         start=True, stop=True).then_inc(S[ready][q], 1)

                def variance(n, src, b, done, ready, updated=None):
                    for q in range(2):
                        wait(done, q, n)
                        if updated is not None:
                            pe.wait_ge(S["st_done"][q], updated)
                        nc.tensor.matmul(bank(q, b)[:, 0:W], c(MEAN, 128, 128), src[q][:, :],
                                         start=True, stop=True).then_inc(S[ready][q], 1)

                def project_qk(n):
                    for q in range(2):
                        wait("xn_done", q, n)
                        nc.tensor.matmul(bank(q, 0)[:, 0:W], lin_w[:, 0, :], xn[q][:, :],
                                         start=True, stop=True).then_inc(S["linq_ready"][q], 1)
                        for i in range(Q):
                            nc.tensor.matmul(bank(q, 1)[0:T, W + 2 * i:W + 2 * i + 2], t(xn, q, i), ab_w[:, :],
                                             start=True, stop=True)
                        nc.tensor.matmul(bank(q, 1)[:, 0:W], lin_w[:, 1, :], xn[q][:, :],
                                         start=True, stop=True).then_inc(S["link_ready"][q], 1)

                def project_vg(n):
                    for q in range(2):
                        wait("linq_done", q, n)
                        nc.tensor.matmul(bank(q, 0)[:, 0:W], lin_w[:, 2, :], xn[q][:, :],
                                         start=True, stop=True).then_inc(S["linv_ready"][q], 1)
                        wait("link_done", q, n)
                        wait("zab_done", q, n)
                        nc.tensor.matmul(bank(q, 1)[:, 0:W], lin_w[:, 3, :], xn[q][:, :],
                                         start=True, stop=True).then_inc(S["gate_ready"][q], 1)

                def decays(n):
                    for q in range(2):
                        wait("gl_done", q, n)
                        wait("linv_done", q, n)
                        nc.tensor.matmul(bank(q, 0)[0:T, 0:W], c(TRI_GT, T, T), gl[q][:, :],
                                         start=True, stop=True).then_inc(S["D_ready"][q], 1)
                        wait("gatelin_done", q, n)
                        nc.tensor.matmul(bank(q, 1)[:, 0:W], c(ONES, T, 128), gl[q][:, :],
                                         start=True, stop=True).then_inc(S["cum_ready"][q], 1)

                def norms(n):
                    for q in range(2):
                        wait("sqqk_done", q, n)
                        wait("edec_done", q, n)
                        nc.tensor.matmul(bank(q, 0)[:, 0:W], c(ONES, 128, 128), sqr[q][:, :],
                                         start=True, stop=True).then_inc(S["nq_ready"][q], 1)
                        wait("eg_done", q, n)
                        nc.tensor.matmul(bank(q, 1)[:, 0:W], c(ONES, 128, 128), sq2[q][:, :],
                                         start=True, stop=True).then_inc(S["nk_ready"][q], 1)

                def products(n):
                    for q in range(2):
                        wait("kn_done", q, n)
                        bmm(lambda i: pT(q, 0, i), lambda i: t(act[1], q, i), lambda i: t(act[1], q, i),
                            "kk_ready", q)
                        bmm(lambda i: pT(q, 1, i), lambda i: t(act[1], q, i), lambda i: t(act[0], q, i),
                            "kq_ready", q)

                def right_side(n, o):
                    for q in range(2):
                        wait("ua_done", q, n)
                        for i in range(Q):
                            m = nc.tensor.transpose(pD(q, 0, i), t(act[1], q, i), c(IDENT, 128, 128))
                        m.then_inc(S["kN_ready"][q], 1)
                    for q in range(2):
                        wait("kg_done", q, n)
                        pe.wait_ge(S["st_done"][q], n + o + 1)
                        wait("pt_done", q, n)
                        for i in range(Q):
                            nc.tensor.matmul(pD(q, 1, i), t(act[2], q, i), c(CENTRE, 128, 128),
                                             start=True, stop=False)
                            m = nc.tensor.matmul(pD(q, 1, i), t(kg, q, i), d(st, q, i),
                                                 start=False, stop=True)
                        m.then_inc(S["R_ready"][q], 1)

                def invert_start(n):
                    for q in range(2):
                        wait("ua_done", q, n)
                        wait_last("x2N_done", q, n)
                        for i in range(Q):
                            m = nc.tensor.transpose(pD(q, 2, i)[:, 0:T], ua[q][:, i * 128:i * 128 + T],
                                                    c(IDENT, T, T))
                        m.then_inc(S["P_ready"][q], 1)

                def invert_p(n, lev):
                    for q in range(2):
                        pe.wait_ge(S["inv_done"][q], n * (LEVELS - 1) + lev)
                        if lev > 1:
                            pe.wait_ge(S["P_done"][q], n * (LEVELS - 1) + lev - 1)
                        bmm(lambda i: half(q, 2, i), lambda i: d(ua, q, i)[:, 0:T],
                            lambda i: blocks(d(inv, q, i), lev, 0), "P_ready", q)

                def invert_xy(n, lev):
                    for q in range(2):
                        pe.wait_ge(S["P_done"][q], n * (LEVELS - 1) + lev)
                        pe.wait_ge(S["invT_done"][q], n * LEVELS + lev)
                        if lev == 1:
                            wait_last("h2N_done", q, n)
                        if lev < LEVELS - 1:
                            for i in range(Q):
                                nc.tensor.matmul(half(q, 3, i), d(invT, q, i)[:, 0:T],
                                                 blocks(d(ps, q, i), lev, 0), start=True, stop=True)
                        bmm(lambda i: half(q, 3, i, Q * HW), lambda i: d(ps, q, i)[:, 0:T],
                            lambda i: blocks(d(invT, q, i), lev, 1), "XY_ready", q)

                def solve(n):
                    for q in range(2):
                        pe.wait_ge(S["invT_done"][q], n * LEVELS + LEVELS)
                        wait("rhs_done", q, n)
                        bmm(lambda i: pD(q, 2, i), lambda i: d(invT, q, i)[:, 0:T], lambda i: d(rhs, q, i),
                            "W_ready", q)

                def outputs(n):
                    for q in range(2):
                        wait("qg_done", q, n)
                        wait("u_done", q, n)
                        for i in range(Q):
                            nc.tensor.matmul(pT(q, 3, i, 128), d(st, q, i), t(qg, q, i),
                                             start=True, stop=False)
                            m = nc.tensor.matmul(pT(q, 3, i, 128), d(u, q, i), t(pt, q, i),
                                                 start=False, stop=True)
                        m.then_inc(S["O_ready"][q], 1)
                    for q in range(2):
                        wait("ue_done", q, n)
                        bmm(lambda i: pD(q, 2, i, 128), lambda i: d(kN, q, i), lambda i: d(ue, q, i),
                            "dS_ready", q)

                def project_out(n):
                    for q in range(2):
                        wait("gated_done", q, n)
                        nc.tensor.matmul(bank(q, 3)[:, 0:W], lin_w[:, 4, :], xt[q][:, :],
                                         start=True, stop=True).then_inc(S["y_ready"][q], 1)

                def turn_out(n):
                    for q in range(2):
                        wait("x2_done", q, n)
                        nc.tensor.matmul(bank(q, 3)[0:E, 0:W], wr_sb[:, :], xt[q][:, :],
                                         start=True, stop=True).then_inc(S["lg_ready"][q], 1)
                        for i in range(Q):
                            m = nc.tensor.transpose(pD(q, 2, i), t(xt, q, i), c(IDENT, 128, 128))
                        m.then_inc(S["x2N_ready"][q], 1)
                    for q in range(2):
                        wait("lg_done", q, n)
                        for i in range(Q):
                            m = nc.tensor.transpose(pD(q, 3, i), t(hres, q, i), c(IDENT, 128, 128))
                        m.then_inc(S["h2N_ready"][q], 1)

                give_ahead(pe, "scale_ready", "h2N_ready")
                pe.wait_ge(weights_loaded, 16 * NW)
                pe.wait_ge(cleared, 6)
                def step(n, o, following):
                    invert_start(n)
                    invert_p(n, 1)
                    turn_x(n + 1)
                    invert_xy(n, 1)
                    convolve(n + 1)
                    invert_p(n, 2)
                    invert_xy(n, 2)
                    invert_p(n, 3)
                    spread_scale(n + 1)
                    invert_xy(n, 3)
                    invert_p(n, 4)
                    invert_xy(n, 4)
                    centre(n + 1, hT, 1, "h_done", "xm_ready")
                    invert_p(n, 5)
                    variance(n + 1, sqr, 0, "xmsq_done", "var_ready")
                    invert_xy(n, 5)
                    invert_p(n, 6)
                    project_qk(n + 1)
                    invert_xy(n, 6)
                    solve(n)
                    project_vg(n + 1)
                    outputs(n)
                    decays(n + 1)
                    variance(n, sqt, 2, "osq_done", "ovar_ready", n + o + 2)
                    norms(n + 1)
                    project_out(n)
                    centre(n, hres, 2, "h2_done", "h2m_ready")
                    products(n + 1)
                    variance(n, sqt, 3, "h2sq_done", "h2var_ready")
                    right_side(n + 1, following)
                    turn_out(n)

                n = 0
                turn_x(n)
                convolve(n)
                spread_scale(n)
                centre(n, hT, 1, "h_done", "xm_ready")
                variance(n, sqr, 0, "xmsq_done", "var_ready")
                project_qk(n)
                project_vg(n)
                decays(n)
                norms(n)
                products(n)
                right_side(n, 0)
                with pe.Fori(0, OCT - 1) as o:
                    with pe.Fori(0, CH - 1) as ch:
                        step(o * CH + ch, o, o)
                    step(o * CH + (CH - 1), o, o + 1)
                with pe.Fori(0, CH - 1) as ch:
                    step(ch + (OCT - 1) * CH, OCT - 1, OCT - 1)
                n = OCT * CH - 1
                invert_start(n)
                for lev in range(1, LEVELS):
                    invert_p(n, lev)
                    invert_xy(n, lev)
                solve(n)
                outputs(n)
                variance(n, sqt, 2, "osq_done", "ovar_ready", n + OCT + 1)
                project_out(n)
                centre(n, hres, 2, "h2_done", "h2m_ready")
                variance(n, sqt, 3, "h2sq_done", "h2var_ready")
                turn_out(n)

            @block.scalar
            def _(sc):
                def wait(name, q, n):
                    sc.wait_ge(S[name][q], count(name, n + 1))

                def wait_last(name, q, n):
                    sc.wait_ge(S[name][q], count(name, n))

                def act_(done, q, dst, src, fn, **kw):
                    nc.scalar.activation(dst, src, fn, **kw).then_inc(S[done][q], 1)

                def take_x(n):
                    for q in range(2):
                        wait("xT_ready", q, n)
                        act_("xT_done", q, xT[q][:, :, :],
                             bank(q, 0)[:, 0:Q * XR].rearrange("p (i t) -> p i t", i=Q), ACT.Copy)

                def take_scale(n):
                    for q in range(2):
                        wait("scale_ready", q, n)
                        act_("scale_done", q, scl[q][:, :], bank(q, 1)[:, 0:W], ACT.Copy)

                def tanh(n):
                    nc.scalar.preload_act_table_set(SILU_SET)
                    for q in range(2):
                        wait("v_done", q, n)
                        wait_last("res_done", q, n)
                        act_("tanh_done", q, hT[q][:, :], scl[q][:, :], ACT.Tanh, scale=LAM)

                def square_x(n):
                    for q in range(2):
                        wait("xm_ready", q, n)
                        act_("xmsq_done", q, sqr[q][:, :], bank(q, 1)[:, 0:W], ACT.Square)

                def inverse_root(n, dst, b, ready, ln, root):
                    for q in range(2):
                        wait(ready, q, n)
                        act_(ln, q, dst[q][:, :], bank(q, b)[:, 0:W], ACT.Ln, bias=c(EPS, 128, 1))
                    for q in range(2):
                        wait(ln, q, n)
                        act_(root, q, dst[q][:, :], dst[q][:, :], ACT.Exp, scale=-0.5)

                def take_lin(n, o, js):
                    for j in js:
                        name, b = (("linq", 0), ("link", 1), ("linv", 0))[j]
                        for q in range(2):
                            wait(name + "_ready", q, n)
                            if j == 0:
                                sc.wait_ge(S["halo_done"][q], n + o + 2)
                            act_(name + "_done", q, lin[j][q][:, :, HALO:HALO + T],
                                 bank(q, b)[:, 0:W].rearrange("p (i t) -> p i t", i=Q),
                                 ACT.Identity, bias=v(V_BQ + j))

                def take_logits(n):
                    for q in range(2):
                        wait("link_ready", q, n)
                        act_("zab_done", q, zab[q][:, :, :],
                             bank(q, 1)[0:T, W:W + 2 * Q].rearrange("p (i a) -> p i a", i=Q), ACT.Copy)

                def take_gate(n):
                    nc.scalar.preload_act_table_set(SILU_SET)
                    for q in range(2):
                        wait("gate_ready", q, n)
                        wait_last("res_done", q, n)
                        act_("gatelin_done", q, gate[q][:, :], bank(q, 1)[:, 0:W], ACT.Silu, bias=v(V_BG))

                def silu(n, j):
                    for q in range(2):
                        sc.wait_ge(S["tap_done"][q], (3 * n + j + 1) * HALO + 1)
                        act_("silu_done", q, act[j][q][:, :], act[j][q][:, :], ACT.Silu)

                def log_gates(n):
                    for q in range(2):
                        wait("az_done", q, n)
                        act_("eab_done", q, eab[q][:, :, :], eab[q][:, :, :], ACT.Exp, scale=-1.0)
                    for q in range(2):
                        wait("eab_done", q, n)
                        act_("lab_done", q, eab[q][:, :, :], eab[q][:, :, :], ACT.Ln, bias=1.0)

                def exp_decays(n):
                    for q in range(2):
                        wait("D_ready", q, n)
                        act_("edec_done", q, dec[q][:, :], bank(q, 0)[0:T, 0:W], ACT.Exp)
                        wait("cum_ready", q, n)
                        act_("eg_done", q, eg[q][:, :], bank(q, 1)[:, 0:W], ACT.Exp)
                    for q in range(2):
                        wait("g_done", q, n)
                        act_("beta_done", q, beta[q][:, :], gab[q][:, :, 1], ACT.Exp)

                def inverse_norms(n):
                    for q in range(2):
                        wait("nq_ready", q, n)
                        act_("lnq_done", q, rq[q][:, :], bank(q, 0)[:, 0:W], ACT.Ln,
                             scale=LN_SCALE, bias=c(TINY, 128, 1))
                        wait("nk_ready", q, n)
                        act_("lnk_done", q, rstd[q][:, :], bank(q, 1)[:, 0:W], ACT.Ln,
                             scale=LN_SCALE, bias=c(TINY, 128, 1))
                        wait("lnq_done", q, n)
                        act_("rq_done", q, rq[q][:, :], rq[q][:, :], ACT.Exp, scale=-0.5, bias=c(LNS, 128, 1))
                        wait("lnk_done", q, n)
                        act_("rk_done", q, rstd[q][:, :], rstd[q][:, :], ACT.Exp, scale=-0.5,
                             bias=c(LNS, 128, 1))

                def take_k(n):
                    for q in range(2):
                        wait("kN_ready", q, n)
                        act_("kN_done", q, kN[q][:, :], bank(q, 0)[0:T, :], ACT.Copy)

                def take_rhs(n):
                    for q in range(2):
                        wait("R_ready", q, n)
                        act_("rhs_done", q, rhs[q][:, :], bank(q, 1)[0:T, :], ACT.Copy)

                def take_p(n, lev):
                    for q in range(2):
                        sc.wait_ge(S["P_ready"][q], n * LEVELS + lev + 1)
                        act_("P_done", q, blocks(ps[q][:, :], lev, 0),
                             bank(q, 2)[0:T, 0:Q * HW].rearrange("p (b s) -> p b s", s=1 << lev), ACT.Copy)

                def square_t(n, b, ready, done):
                    for q in range(2):
                        wait(ready, q, n)
                        act_(done, q, sqt[q][:, :], bank(q, b)[:, 0:W], ACT.Square)

                def take_out(n):
                    for q in range(2):
                        wait("lg_ready", q, n)
                        sc.wait_ge(S["lg_stored"][q], 16 * n + 16)
                        act_("lg_done", q, lg[q][:, :], bank(q, 3)[0:E, 0:W], ACT.Copy)
                    for q in range(2):
                        wait("h2N_ready", q, n)
                        sc.wait_ge(S["h2_stored"][q], 16 * n + 16)
                        act_("h2N_done", q, h2N[q][:, :], bank(q, 3)[0:T, :], ACT.Copy)

                sc.wait_ge(weights_loaded, 16 * NW)
                give_ahead(sc, "h2N_done", "rhs_done")
                sc.wait_ge(cleared, 6)
                def step(n, o, following):
                    take_p(n, 1)
                    take_x(n + 1)
                    take_p(n, 2)
                    take_p(n, 3)
                    take_scale(n + 1)
                    tanh(n + 1)
                    take_p(n, 4)
                    nc.scalar.preload_act_table_set(LOG_SET)
                    square_x(n + 1)
                    take_p(n, 5)
                    inverse_root(n + 1, rstd, 0, "var_ready", "lnv_done", "rstd_done")
                    take_p(n, 6)
                    take_lin(n + 1, following, (0, 1))
                    take_logits(n + 1)
                    log_gates(n + 1)
                    take_lin(n + 1, following, (2,))
                    take_gate(n + 1)
                    silu(n + 1, 0)
                    silu(n + 1, 1)
                    square_t(n, 3, "O_ready", "osq_done")
                    silu(n + 1, 2)
                    nc.scalar.preload_act_table_set(LOG_SET)
                    exp_decays(n + 1)
                    inverse_root(n, rst, 2, "ovar_ready", "lno_done", "rstdo_done")
                    inverse_norms(n + 1)
                    square_t(n, 2, "h2m_ready", "h2sq_done")
                    inverse_root(n, rst, 3, "h2var_ready", "lnh2_done", "rstdh2_done")
                    take_k(n + 1)
                    take_rhs(n + 1)
                    take_out(n)

                n = 0
                take_x(n)
                take_scale(n)
                tanh(n)
                square_x(n)
                nc.scalar.preload_act_table_set(LOG_SET)
                inverse_root(n, rstd, 0, "var_ready", "lnv_done", "rstd_done")
                take_lin(n, 0, (0, 1))
                take_logits(n)
                log_gates(n)
                take_lin(n, 0, (2,))
                take_gate(n)
                for j in range(3):
                    silu(n, j)
                nc.scalar.preload_act_table_set(LOG_SET)
                exp_decays(n)
                inverse_norms(n)
                take_k(n)
                take_rhs(n)
                with sc.Fori(0, OCT - 1) as o:
                    with sc.Fori(0, CH - 1) as ch:
                        step(o * CH + ch, o, o)
                    step(o * CH + (CH - 1), o, o + 1)
                with sc.Fori(0, CH - 1) as ch:
                    step(ch + (OCT - 1) * CH, OCT - 1, OCT - 1)
                n = OCT * CH - 1
                for lev in range(1, LEVELS):
                    take_p(n, lev)
                square_t(n, 3, "O_ready", "osq_done")
                inverse_root(n, rst, 2, "ovar_ready", "lno_done", "rstdo_done")
                square_t(n, 2, "h2m_ready", "h2sq_done")
                inverse_root(n, rst, 3, "h2var_ready", "lnh2_done", "rstdh2_done")
                take_out(n)

            @block.vector
            def _(ve):
                def reg(value):
                    return value if isinstance(value, int) else ve.to_reg(ve.snap(value))

                def wait(name, q, n):
                    ve.wait_ge(S[name][q], count(name, n + 1))

                def wait_value(q, name, value):
                    value = reg(value)
                    ve.wait_ge(masks_loaded, 16)
                    ve.wait_ge(S[name][q], value)

                def inc(ins, name, q):
                    ins.then_inc(S[name][q], 1)

                def sum_squares(n):
                    for q in range(2):
                        wait("xsq_done", q, n)
                        inc(nc.vector.reduce_sum(ssq[q][:, :], xsq[q][:, :, :], X), "ssq_done", q)

                def window_sum(n):
                    for q in range(2):
                        wait("wsum_ready", q, n)
                        inc(nc.vector.tensor_scalar(wcol[q][:, :], bank(q, 1)[0:T, 0:Q], 0.0, None, ALU.max),
                            "wmax_done", q)

                def window_scale(n):
                    for q in range(2):
                        wait("wroot_done", q, n)
                        inc(nc.vector.tensor_scalar(wcol[q][:, :], wcol[q][:, :], 1e-7, None, ALU.add),
                            "weps_done", q)
                    for q in range(2):
                        wait("weps_done", q, n)
                        inc(nc.vector.reciprocal(wcol[q][:, :], wcol[q][:, :]), "wrec_done", q)
                    for q in range(2):
                        wait("wrec_done", q, n)
                        inc(nc.vector.tensor_scalar(wcol[q][:, :], wcol[q][:, :], 1.0, None, ALU.min),
                            "wcol_done", q)

                def scale(n):
                    for q in range(2):
                        wait("conv_ready", q, n)
                        wait("scale_done", q, n)
                        inc(nc.vector.tensor_tensor(scl[q][:, :], bank(q, 0)[:, 0:W], scl[q][:, :], ALU.mult),
                            "v_done", q)

                def tokens(n):
                    for q in range(2):
                        wait("tanh_done", q, n)
                        inc(nc.vector.tensor_scalar(hT[q][:, :], hT[q][:, :], v(V_TOKB), 0.0, ALU.add, ALU.max),
                            "h_done", q)

                def norm_x(n):
                    for q in range(2):
                        wait("rstd_done", q, n)
                        inc(nc.vector.tensor_tensor(xn[q][:, :], bank(q, 1)[:, 0:W], rstd[q][:, :], ALU.mult),
                            "xn_done", q)

                def gate_logits(n):
                    for q in range(2):
                        wait("zab_done", q, n)
                        inc(nc.vector.tensor_tensor(zab[q][:, :, :], zab[q][:, :, :],
                                                    over(ab_b[0:T, :], 2), ALU.add), "z_done", q)
                    for q in range(2):
                        wait("z_done", q, n)
                        inc(nc.vector.tensor_scalar(nab[q][:, :, :], zab[q][:, :, :], -1.0, None, ALU.mult),
                            "nz_done", q)
                    for q in range(2):
                        wait("nz_done", q, n)
                        inc(nc.vector.tensor_tensor(eab[q][:, :, :], zab[q][:, :, :], nab[q][:, :, :], ALU.max),
                            "az_done", q)
                    for q in range(2):
                        wait("az_done", q, n)
                        inc(nc.vector.tensor_scalar(nab[q][:, :, :], zab[q][:, :, :], 0.0, None, ALU.min),
                            "mab_done", q)

                def taps(n, j):
                    for k in range(1, DW):
                        for q in range(2):
                            if k == 1:
                                ve.wait_ge(S["tap0_done"][q], 3 * n + j + 1)
                            else:
                                ve.wait_ge(S["tap_done"][q], (3 * n + j) * HALO + k)
                            inc(nc.vector.scalar_tensor_tensor(
                                tiles(act[j][q]), lin[j][q][:, :, k:k + T], v(V_CW + DW * j + k),
                                tiles(act[j][q]), ALU.mult, ALU.add), "tap_done", q)

                def gates(n):
                    for q in range(2):
                        wait("lab_done", q, n)
                        wait("mab_done", q, n)
                        inc(nc.vector.tensor_tensor(gab[q][:, :, :], nab[q][:, :, :], eab[q][:, :, :],
                                                    ALU.subtract), "g_done", q)

                def units(n):
                    for q in range(2):
                        wait("rq_done", q, n)
                        inc(nc.vector.scalar_tensor_tensor(act[0][q][:, :], rq[q][:, :], 1e12,
                                                           act[0][q][:, :], ALU.min, ALU.mult), "qn_done", q)
                        wait("rk_done", q, n)
                        inc(nc.vector.scalar_tensor_tensor(act[1][q][:, :], rstd[q][:, :], 1e12,
                                                           act[1][q][:, :], ALU.min, ALU.mult), "kn_done", q)
                    for q in range(2):
                        wait("kn_done", q, n)
                        wait("eg_done", q, n)
                        inc(nc.vector.scalar_tensor_tensor(kg[q][:, :], act[1][q][:, :], -1.0, eg[q][:, :],
                                                           ALU.mult, ALU.mult), "kg_done", q)

                def system(n):
                    for q in range(2):
                        wait("kk_ready", q, n)
                        wait("eb_done", q, n)
                        inc(nc.vector.tensor_tensor(
                            tiles(ua[q], 128)[:, :, 0:T], bank(q, 0)[0:T, 0:W].rearrange("p (i t) -> p i t", i=Q),
                            tiles(eb[q]), ALU.mult), "ua_done", q)
                        wait("kq_ready", q, n)
                        inc(nc.vector.tensor_tensor(pt[q][:, :], bank(q, 1)[0:T, 0:W], dec[q][:, :], ALU.mult),
                            "pt_done", q)

                def merge(dst, src, lev, odd):
                    at = MASKS + (2 * lev + odd) * Q * HW
                    mask = c(at, T, Q * HW).bitcast(i32).rearrange("p (b s) -> p b s", s=1 << lev)
                    return nc.vector.copy_predicated(blocks(dst[:, :], lev, odd), mask, src)

                def merge_start(n):
                    for q in range(2):
                        eye, there = (reg(count(name, n + 1)) for name in ("eye_done", "ua_done"))
                        ve.wait_ge(masks_loaded, 16)
                        ve.wait_ge(S["ua_done"][q], there)
                        ve.wait_ge(S["eye_done"][q], eye)
                        inc(merge(invT[q], blocks(ua[q][:, :], 0, 1), 0, 1), "invT_done", q)
                    for q in range(2):
                        wait_value(q, "P_ready", n * LEVELS + 1)
                        inc(merge(inv[q], blocks(bank(q, 2)[0:T, :], 0, 0), 0, 0), "inv_done", q)

                def merges(n, lev):
                    def packed(q, at):
                        return bank(q, 3)[0:T, at:at + Q * HW].rearrange("p (b s) -> p b s", s=1 << lev)

                    for q in range(2):
                        wait_value(q, "XY_ready", n * (LEVELS - 1) + lev)
                        if lev < LEVELS - 1:
                            inc(merge(inv[q], packed(q, 0), lev, 0), "inv_done", q)
                        inc(merge(invT[q], packed(q, Q * HW), lev, 1), "invT_done", q)

                def updates(n):
                    for q in range(2):
                        wait("W_ready", q, n)
                        inc(nc.vector.tensor_tensor(tiles(u[q], 128),
                                                    bank(q, 2)[0:T, :].rearrange("p (i d) -> p i d", i=Q),
                                                    along(beta[q][:, :], 128), ALU.mult), "u_done", q)

                def state(n):
                    for q in range(2):
                        wait("decay_st_done", q, n)
                        wait("dS_ready", q, n)
                        inc(nc.vector.tensor_tensor(st[q][:, :], bank(q, 2)[:, :], st[q][:, :], ALU.add),
                            "st_done", q)

                def norm_out(n):
                    for q in range(2):
                        wait("rstdo_done", q, n)
                        inc(nc.vector.tensor_tensor(xt[q][:, :], bank(q, 3)[:, 0:W], rst[q][:, :], ALU.mult),
                            "on_done", q)
                    for q in range(2):
                        wait("on_done", q, n)
                        wait("res_done", q, n)
                        inc(nc.vector.tensor_tensor(xt[q][:, :], xt[q][:, :], gn[q][:, :], ALU.mult),
                            "gated_done", q)

                def residual(n):
                    for q in range(2):
                        wait("y_ready", q, n)
                        inc(nc.vector.scalar_tensor_tensor(hres[q][:, :], bank(q, 3)[:, 0:W], v(V_BO),
                                                           hres[q][:, :], ALU.add, ALU.add), "h2_done", q)

                def norm_h2(n):
                    for q in range(2):
                        wait("rstdh2_done", q, n)
                        inc(nc.vector.tensor_tensor(xt[q][:, :], bank(q, 2)[:, 0:W], rst[q][:, :], ALU.mult),
                            "x2_done", q)

                def take_x2(n):
                    for q in range(2):
                        wait("x2N_ready", q, n)
                        ve.wait_ge(S["x2_stored"][q], 16 * n + 16)
                        inc(nc.vector.tensor_copy(x2N[q][:, :], bank(q, 2)[0:T, :]), "x2N_done", q)

                ve.wait_ge(weights_loaded, 16 * NW)
                give_ahead(ve, "ssq_done", "x2N_done", "tap_done")
                for q in range(2):
                    nc.vector.memset(ua[q][:, :], 0.0).then_inc(cleared, 1)
                    nc.vector.memset(ps[q][:, :], 0.0).then_inc(cleared, 1)
                    nc.vector.memset(bank(q, 2)[0:T, :], 0.0).then_inc(cleared, 1)
                ve.wait_ge(cleared, 6)
                def clear_state(updates):
                    for q in range(2):
                        ve.wait_ge(S["st_done"][q], updates)
                        nc.vector.memset(st[q][:, :], 0.0).then_inc(S["st_done"][q], 1)

                def step(n, o, following):
                    merge_start(n)
                    sum_squares(n + 1)
                    merges(n, 1)
                    window_sum(n + 1)
                    merges(n, 2)
                    window_scale(n + 1)
                    scale(n + 1)
                    merges(n, 3)
                    tokens(n + 1)
                    merges(n, 4)
                    merges(n, 5)
                    norm_x(n + 1)
                    merges(n, 6)
                    gate_logits(n + 1)
                    taps(n + 1, 0)
                    updates(n)
                    gates(n + 1)
                    taps(n + 1, 1)
                    state(n)
                    if following is not o:
                        clear_state(n + o + 2)
                    taps(n + 1, 2)
                    norm_out(n)
                    residual(n)
                    units(n + 1)
                    system(n + 1)
                    norm_h2(n)
                    take_x2(n)

                for q in range(2):
                    nc.vector.memset(st[q][:, :], 0.0).then_inc(S["st_done"][q], 1)
                n = 0
                sum_squares(n)
                window_sum(n)
                window_scale(n)
                scale(n)
                tokens(n)
                norm_x(n)
                gate_logits(n)
                taps(n, 0)
                gates(n)
                taps(n, 1)
                taps(n, 2)
                units(n)
                system(n)
                with ve.Fori(0, OCT - 1) as o:
                    with ve.Fori(0, CH - 1) as ch:
                        step(o * CH + ch, o, o)
                    step(o * CH + (CH - 1), o, o + 1)
                with ve.Fori(0, CH - 1) as ch:
                    step(ch + (OCT - 1) * CH, OCT - 1, OCT - 1)
                n = OCT * CH - 1
                merge_start(n)
                for lev in range(1, LEVELS):
                    merges(n, lev)
                updates(n)
                state(n)
                norm_out(n)
                residual(n)
                norm_h2(n)
                take_x2(n)

            @block.gpsimd
            def _(po):
                def reg(value):
                    return value if isinstance(value, int) else po.to_reg(po.snap(value))

                def wait(name, q, n):
                    po.wait_ge(S[name][q], count(name, n + 1))

                def wait_value(q, name, value):
                    value = reg(value)
                    po.wait_ge(weights_loaded, 16 * NW)
                    po.wait_ge(S[name][q], value)

                def inc(ins, name, q):
                    ins.then_inc(S[name][q], 1)

                def squares(n):
                    for q in range(2):
                        po.wait_ge(S["xin_loaded"][q], 32 * n + 32)
                        po.wait_ge(S["ssq_done"][q], n + 1)
                        inc(nc.gpsimd.tensor_tensor(xsq[q][:, :, :], xin[q][:, :, 0:CIN], xin[q][:, :, 0:CIN],
                                                    ALU.mult), "xsq_done", q)

                def window_root(n):
                    for q in range(2):
                        wait("wmax_done", q, n)
                        inc(nc.gpsimd.tensor_tensor(wcol[q][:, :], wcol[q][:, :],
                                                    c(HALF, T, 1).to_broadcast([T, Q]), ALU.pow),
                            "wroot_done", q)

                def first_taps(n, js):
                    for j in js:
                        name = ("linq", "link", "linv")[j]
                        for q in range(2):
                            wait_value(q, name + "_done", count(name + "_done", n + 1))
                            inc(nc.gpsimd.tensor_scalar(tiles(act[j][q]), lin[j][q][:, :, 0:T],
                                                        v(V_CW + DW * j), v(V_CB + j), ALU.mult, ALU.add),
                                "tap0_done", q)

                def log_decays(n):
                    for q in range(2):
                        wait("g_done", q, n)
                        inc(nc.gpsimd.tensor_tensor(tiles(gl[q]), over(c(TRI_LE, T, T)),
                                                    along(gab[q][:, :, 0], T), ALU.mult), "gl_done", q)

                def squares_qk(n):
                    for q in range(2):
                        po.wait_ge(S["silu_done"][q], 3 * n + 2)
                        nc.gpsimd.tensor_tensor(sqr[q][:, :], act[0][q][:, :], act[0][q][:, :], ALU.mult)
                        inc(nc.gpsimd.tensor_tensor(sq2[q][:, :], act[1][q][:, :], act[1][q][:, :], ALU.mult),
                            "sqqk_done", q)

                def decays(n):
                    for q in range(2):
                        wait("edec_done", q, n)
                        inc(nc.gpsimd.tensor_tensor(tiles(dec[q]), tiles(dec[q]), over(c(TRI_LE, T, T)),
                                                    ALU.mult), "dec_done", q)
                    for q in range(2):
                        wait_value(q, "beta_done", count("beta_done", n + 1))
                        inc(nc.gpsimd.tensor_scalar(nbeta[q][:, :], beta[q][:, :], -1.0, 0.0, ALU.mult, ALU.add),
                            "nbeta_done", q)
                    for q in range(2):
                        wait("dec_done", q, n)
                        wait("nbeta_done", q, n)
                        inc(nc.gpsimd.tensor_tensor(tiles(eb[q]), tiles(dec[q]), along(nbeta[q][:, :], T),
                                                    ALU.mult), "eb_done", q)

                def starts(n):
                    for q in range(2):
                        wait("qn_done", q, n)
                        wait("eg_done", q, n)
                        inc(nc.gpsimd.tensor_tensor(qg[q][:, :], act[0][q][:, :], eg[q][:, :], ALU.mult),
                            "qg_done", q)
                        for k in (inv, invT):
                            ins = nc.gpsimd.tensor_scalar(tiles(k[q], 128), over(c(IDENT, T, 128), 128), 1.0, 0.0,
                                                          ALU.mult, ALU.add)
                        inc(ins, "eye_done", q)

                def move_halo(n):
                    for q in range(2):
                        wait_value(q, "tap_done", 3 * HALO * (n + 1) + 1)
                        for j in range(3):
                            ins = nc.gpsimd.tensor_copy(lin[j][q][:, :, 0:HALO], lin[j][q][:, :, T:T + HALO])
                        inc(ins, "halo_done", q)

                def keep(n):
                    for q in range(2):
                        wait_value(q, "h2N_ready", count("h2N_ready", n))
                        nc.gpsimd.tensor_scalar(hres[q][:, :], hT[q][:, :], 1.0, 0.0, ALU.mult, ALU.add)
                        inc(nc.gpsimd.tensor_scalar(gn[q][:, :], gate[q][:, :], v(V_NORM), 0.0, ALU.mult, ALU.add),
                            "res_done", q)

                def decay_state(n):
                    for q in range(2):
                        wait("u_done", q, n)
                        inc(nc.gpsimd.tensor_tensor(tiles(ue[q], 128), tiles(u[q], 128),
                                                    along(tiles(dec[q])[:, :, T - 1], 128), ALU.mult),
                            "ue_done", q)
                    for q in range(2):
                        wait("O_ready", q, n)
                        inc(nc.gpsimd.tensor_tensor(tiles(st[q], 128), tiles(st[q], 128),
                                                    along(tiles(eg[q])[:, :, T - 1], 128), ALU.mult),
                            "decay_st_done", q)

                give_ahead(po, "xsq_done", "res_done", "halo_done")
                po.wait_ge(weights_loaded, 16 * NW)
                def clear_halo(o):
                    for q in range(2):
                        tapped, moved = reg(o * (CH * 3 * HALO) + 1), reg(o * (CH + 1) + 1)
                        po.wait_ge(weights_loaded, 16 * NW)
                        po.wait_ge(S["tap_done"][q], tapped)
                        po.wait_ge(S["halo_done"][q], moved)
                        for j in range(3):
                            ins = nc.gpsimd.memset(lin[j][q][:, :, 0:HALO], 0.0)
                        ins.then_inc(S["halo_done"][q], 1)

                def step(n, o, following):
                    if following is not o:
                        clear_halo(following)
                    squares(n + 1)
                    window_root(n + 1)
                    first_taps(n + 1, (0, 1, 2))
                    decay_state(n)
                    log_decays(n + 1)
                    squares_qk(n + 1)
                    decays(n + 1)
                    starts(n + 1)
                    move_halo(n + 1)
                    keep(n + 1)

                clear_halo(0)
                n = 0
                squares(n)
                window_root(n)
                first_taps(n, (0, 1, 2))
                log_decays(n)
                squares_qk(n)
                decays(n)
                starts(n)
                move_halo(n)
                keep(n)
                with po.Fori(0, OCT - 1) as o:
                    with po.Fori(0, CH - 1) as ch:
                        step(o * CH + ch, o, o)
                    step(o * CH + (CH - 1), o, o + 1)
                with po.Fori(0, CH - 1) as ch:
                    step(ch + (OCT - 1) * CH, OCT - 1, OCT - 1)
                n = OCT * CH - 1
                decay_state(n)


def experts_phase(nc, banks, cst, wr_sb, w1, b1, w2, b2, out, x2_rows, logits,
                  f32, bf16, i32, u32, ACT, X):
    PAIRS = E // 2
    FC = FF // 128
    TB = CH * B
    PX = 2 * TB
    ROUNDS = 15
    HALF_T = ST // 2
    ctx = ExitStack()
    with ctx:
        def sb(name, shape, dt=f32):
            return ctx.enter_context(nc.sbuf_tensor(name, shape, dt))

        def sem(name):
            return ctx.enter_context(nc.semaphore(name))

        lgt = sb("lgt", [128, L])
        dist = sb("dist", [128, L])
        scan_one = sb("scan_one", [128, L])
        work = sb("work", [128, L])
        below = sb("below", [128, L])
        ties = sb("ties", [128, L])
        chosen = sb("chosen", [128, L])
        slot = sb("slot", [128, L])
        sloti = sb("sloti", [128, L], i32)
        hii = sb("hii", [128, L], i32)
        loi = sb("loi", [128, L], i32)
        hib = sb("hib", [128, L], bf16)
        lob = sb("lob", [128, L], bf16)
        rowmax = sb("rowmax", [128, 1])
        gmax = sb("gmax", [1, E])
        gspread = sb("gspread", [1, 128])
        mx = sb("mx", [128, 1])
        rowsum = sb("rowsum", [128, 1])
        zcol = sb("zcol", [128, 1])
        nmxb = sb("nmxb", [128, E])
        rzb = sb("rzb", [128, E])
        kth = sb("kth", [128, 1], i32)
        bits = sb("bits", [128, 3], i32)
        low = sb("low", [128, 1])
        cand = sb("cand", [128, 3], i32)
        keep = sb("keep", [128, 3])
        kept = sb("kept", [128, 1])
        gain = sb("gain", [128, 1], i32)
        cnt = sb("cnt", [128, 3])
        nbelow = sb("nbelow", [128, 1])
        col = sb("col", [128, 3])
        identb = sb("identb", [128, 128], bf16)
        tile_no = sb("tile_no", [T, PX], bf16)
        hiT = sb("hiT", [T, E * TB], bf16)
        loT = sb("loT", [T, E * TB], bf16)
        hot_hi = sb("hot_hi", [T, HI, PX], bf16)
        hot_lo = sb("hot_lo", [T, 3 * LO, PX], bf16)
        found = sb("found", [HI, 2, 2, LO])
        ids = sb("ids", [HI, 2, LO], u32)
        idx_next = sb("idx_next", [128, 2, ST], u32)
        idx = sb("idx", [128, 2, ST], u32)
        w1s = [sb(f"w1s{j}", [128, FF]) for j in range(2)]
        w2s = [sb(f"w2s{j}", [128, FC, F]) for j in range(2)]
        b1s = [sb(f"b1s{j}", [128, FC]) for j in range(2)]
        b2s = [sb(f"b2s{j}", [128, F]) for j in range(2)]
        cur = sb("cur", [128, 3, 2])
        xs = [sb(f"xs{j}", [128, ST, F]) for j in range(2)]
        xsT = [sb(f"xsT{j}", [128, ST * 128]) for j in range(2)]
        val = sb("val", [128, 2, ST])
        hid = [sb(f"hid{i}", [128, HALF_T * 128]) for i in range(2 * FC)]
        y = [sb(f"y{i}", [128, HALF_T, F]) for i in range(2)]

        logits_in, consts_in = sem("logits_in"), sem("consts_in")
        rowmax_done, rowmax_ready, gmax_done, spread_done = map(sem, ("rowmax_done", "rowmax_ready", "gmax_done", "spread_done"))
        mx_ready, mx_done, dist_done, rowsum_done = map(sem, ("mx_ready", "mx_done", "dist_done", "rowsum_done"))
        z_ready, z_done, stats_ready, stats_done = map(sem, ("z_ready", "z_done", "stats_ready", "stats_done"))
        cand_done, cnt_done, total_ready, keep_done, gain_done, kth_done, bit_done = map(
            sem, ("cand_done", "cnt_done", "total_ready", "keep_done", "gain_done", "kth_done", "bit_done"))
        pick_step, ties_ready, offset_ready, split_ready, splitT_done = map(
            sem, ("pick_step", "ties_ready", "offset_ready", "split_ready", "splitT_done"))
        hot_done, scaled_done, list_ready, found_done, ids_done, idx_in = map(
            sem, ("hot_done", "scaled_done", "list_ready", "found_done", "ids_done", "idx_in"))
        idx_done, cur_done, val_ready, exp_done, val_done = map(
            sem, ("idx_done", "cur_done", "val_ready", "exp_done", "val_done"))
        gathered = [sem(f"gathered{j}") for j in range(2)]
        weights_in = [sem(f"weights_in{j}") for j in range(2)]
        xsT_ready, xsT_done, hid_ready, hid_done, y_ready, y_done, yw_done, scattered = map(
            sem, ("xsT_ready", "xsT_done", "hid_ready", "hid_done", "y_ready", "ysum_done", "yw_done", "scattered"))

        def c(at, rows, cols):
            return cst[0:rows, at:at + cols]

        PER = 2 * 2

        with nc.Block() as block:

            @block.sync
            def _(sp):
                sp.dma_start(lgt[:, :], logits.rearrange("e b t -> (e b) t")).then_inc(logits_in, 16)

                def weights(k):
                    for j in range(2):
                        e = bass.ds(2 * k + j, 1)
                        used = sp.to_reg(sp.snap(PER * k + 2))
                        sp.wait_ge(y_ready, used)
                        sp.wait_ge(y_done, used)
                        sp.dma_start(w1s[j][:, :], w1[e, :, :].rearrange("e d f -> d (e f)")).then_inc(weights_in[j], 16)
                        sp.dma_start(w2s[j][:, :, :], w2[e, :, :].rearrange("e (c p) d -> p (e c) d", c=FC))\
                            .then_inc(weights_in[j], 16)
                        sp.dma_start(b1s[j][:, :], b1[:, e, :].rearrange("p e c -> p (e c)")).then_inc(weights_in[j], 16)
                        sp.dma_start(b2s[j][:, :], b2[bass.ds((2 * k + j) * F, F)].partition_broadcast(128))\
                            .then_inc(weights_in[j], 16)

                def indices(k):
                    listed, copied = sp.to_reg(sp.snap(k + 1)), sp.to_reg(sp.snap(k + 1))
                    sp.wait_ge(ids_done, listed)
                    sp.wait_ge(idx_done, copied)
                    for h in range(2):
                        sp.dma_start(idx_next[HI * h:HI * (h + 1), :, :], ids[:, :, ST * h:ST * (h + 1)])\
                            .then_inc(idx_in, 16)

                sp.sem_inc(idx_done, 1)
                indices(0)
                weights(0)
                with sp.Fori(0, PAIRS - 1) as k:
                    indices(k + 1)
                    weights(k + 1)

            @block.tensor
            def _(pe):
                pe.wait_ge(rowmax_done, 1)
                nc.tensor.transpose(banks[0][0:1, 0:128], rowmax[:, :], c(IDENT, 128, 128)).then_inc(rowmax_ready, 1)
                pe.wait_ge(spread_done, 1)
                nc.tensor.matmul(banks[1][:, 0:1], gspread[:, :], c(ONES, 1, 1), start=True, stop=True)\
                    .then_inc(mx_ready, 1)
                pe.wait_ge(rowsum_done, 1)
                nc.tensor.matmul(banks[2][:, 0:1], c(GROUP, 128, 128), rowsum[:, :], start=True, stop=True)\
                    .then_inc(z_ready, 1)
                pe.wait_ge(z_done, 1)
                nc.tensor.matmul(banks[3][:, 0:E], mx[:, 0:1].to_broadcast([128, 128]), c(PICK, 128, E),
                                 start=True, stop=True)
                nc.tensor.matmul(banks[3][:, E:2 * E], zcol[:, 0:1].to_broadcast([128, 128]), c(PICK, 128, E),
                                 start=True, stop=True).then_inc(stats_ready, 1)
                with pe.Fori(0, ROUNDS) as r:
                    pe.wait_ge(cnt_done, r + 1)
                    nc.tensor.matmul(banks[0][:, 0:3], c(GROUP, 128, 128), cnt[:, :], start=True, stop=True)\
                        .then_inc(total_ready, 1)
                pe.wait_ge(cnt_done, ROUNDS + 1)
                nc.tensor.matmul(banks[0][:, 0:1], c(GROUP, 128, 128), cnt[:, 0:1], start=True, stop=True)\
                    .then_inc(total_ready, 1)
                pe.wait_ge(pick_step, 3)
                nc.tensor.matmul(banks[1][:, 0:1], c(GROUP, 128, 128), nbelow[:, :], start=True, stop=True)
                nc.tensor.matmul(banks[1][:, 1:2], c(EARLIER, 128, 128), work[:, L - 1:L], start=True, stop=True)\
                    .then_inc(ties_ready, 1)
                pe.wait_ge(pick_step, 9)
                nc.tensor.matmul(banks[2][:, 0:1], c(EARLIER, 128, 128), slot[:, L - 1:L], start=True, stop=True)\
                    .then_inc(offset_ready, 1)
                pe.wait_ge(pick_step, 16)
                for s, src in enumerate((hib, lob)):
                    for ch in range(CH):
                        m = nc.tensor.transpose(
                            banks[3 + 2 * s + ch // 4][0:T, :].bitcast(bf16)[:, (ch % 4) * 128:(ch % 4 + 1) * 128],
                            src[:, ch * T:(ch + 1) * T], identb[:, :])
                m.then_inc(split_ready, 1)

                def lists(k):
                    pe.wait_ge(hot_done, k + 1)
                    pe.wait_ge(scaled_done, 2 * k + 2)
                    for j in range(2):
                        for t in range(TB):
                            at = j * TB + t
                            m = nc.tensor.matmul(banks[6][0:HI, 2 * LO * j:2 * LO * (j + 1)], hot_hi[:, :, at],
                                                 hot_lo[:, LO:3 * LO, at], start=(t == 0), stop=(t == TB - 1))
                    m.then_inc(list_ready, 1)

                def turn(k):
                    for j in range(2):
                        pe.wait_ge(gathered[j], 16 * ST * k + 16 * ST)
                        for h in range(2):
                            pe.wait_ge(xsT_done, PER * k + 2 * j + h + 1)
                            for g in range(HALF_T):
                                m = nc.tensor.transpose(banks[h][:, g * 128:(g + 1) * 128],
                                                        xs[j][:, HALF_T * h + g, :], c(IDENT, 128, 128))
                            m.then_inc(xsT_ready, 1)
                    pe.wait_ge(cur_done, k + 1)
                    pe.wait_ge(xsT_done, PER * k + 6)
                    for j in range(2):
                        for g in range(ST):
                            m = nc.tensor.matmul(banks[7][:, ST * j + g:ST * j + g + 1],
                                                 xsT[j][:, g * 128:(g + 1) * 128], cur[:, 2, j:j + 1],
                                                 start=True, stop=True)
                    m.then_inc(val_ready, 1)

                def expert(k, j):
                    pe.wait_ge(weights_in[j], 64 * k + 64)
                    for h in range(2):
                        for f in range(FC):
                            pe.wait_ge(hid_done, (2 * k + j) * 2 * FC + h * FC + f + 1)
                            nc.tensor.matmul(banks[2 + f % 2][:, :], w1s[j][:, f * 128:(f + 1) * 128],
                                             xsT[j][:, h * 512:(h + 1) * 512], start=True, stop=True)\
                                .then_inc(hid_ready, 1)
                    for h in range(2):
                        pe.wait_ge(hid_done, (2 * k + j) * 2 * FC + (h + 1) * FC + 2)
                        pe.wait_ge(y_done, (2 * k + j) * 2 + h + 1)
                        for g in range(HALF_T):
                            for f in range(FC):
                                m = nc.tensor.matmul(banks[4 + h][:, g * 128:(g + 1) * 128],
                                                     hid[h * FC + f][:, g * 128:(g + 1) * 128], w2s[j][:, f, :],
                                                     start=(f == 0), stop=(f == FC - 1))
                        m.then_inc(y_ready, 1)

                pe.sem_inc(y_ready, 2)
                pe.sem_inc(list_ready, 1)
                pe.wait_ge(splitT_done, 1)
                lists(0)
                lists(1)
                with pe.Fori(0, PAIRS - 2) as k:
                    turn(k)
                    expert(k, 0)
                    lists(k + 2)
                    expert(k, 1)
                with pe.Fori(PAIRS - 2, PAIRS) as k:
                    turn(k)
                    expert(k, 0)
                    expert(k, 1)

            @block.scalar
            def _(sc):
                nc.scalar.preload_act_table_set(LOG_SET)
                sc.wait_ge(dist_done, 1)
                nc.scalar.activation(work[:, :], dist[:, :], ACT.Exp, scale=-1.0, accum_out=rowsum[:, :])\
                    .then_inc(rowsum_done, 1)

                def values(k):
                    sc.wait_ge(val_ready, k + 1)
                    sc.wait_ge(val_done, k + 1)
                    sc.wait_ge(yw_done, PER * k + 1)
                    for j in range(2):
                        m = nc.scalar.activation(val[:, j, :], banks[7][:, ST * j:ST * (j + 1)], ACT.Exp,
                                                 bias=cur[:, 0, j:j + 1])
                    m.then_inc(exp_done, 1)

                def expert(k, j):
                    for h in range(2):
                        for f in range(FC):
                            sc.wait_ge(hid_ready, (2 * k + j) * 2 * FC + h * FC + f + 1)
                            if f == 0:
                                sc.wait_ge(y_ready, (2 * k + j) * 2 + h + 1)
                            nc.scalar.activation(hid[h * FC + f][:, :], banks[2 + f % 2][:, :], ACT.Gelu,
                                                 bias=b1s[j][:, f:f + 1]).then_inc(hid_done, 1)

                sc.sem_inc(hid_done, 2)
                with sc.Fori(0, PAIRS) as k:
                    values(k)
                    for j in range(2):
                        expert(k, j)

            @block.vector
            def _(ve):
                ve.wait_ge(logits_in, 16)
                nc.vector.tensor_copy(identb[:, :], c(IDENT, 128, 128))
                nc.vector.tensor_copy(tile_no[:, :], c(TILE_NO, T, PX))
                nc.vector.memset(scan_one[:, :], 1.0)
                nc.vector.memset(kth[:, :], 0).then_inc(kth_done, 1)
                for i in range(3):
                    nc.vector.memset(bits[:, i:i + 1], (i + 1) << (2 * ROUNDS - 1))
                nc.vector.memset(low[:, :], float(1 << (2 * ROUNDS - 1))).then_inc(bit_done, 1)
                nc.vector.reduce_max(rowmax[:, :], lgt[:, :], X).then_inc(rowmax_done, 1)
                ve.wait_ge(rowmax_ready, 1)
                nc.vector.reduce_max(gmax[:, :], banks[0][0:1, 0:128].rearrange("p (e b) -> p e b", e=E), X)\
                    .then_inc(gmax_done, 1)
                ve.wait_ge(gmax_done, 1)
                nc.vector.tensor_copy(gspread[:, :].rearrange("p (e b) -> p e b", e=E),
                                      gmax[:, :].unsqueeze(2).to_broadcast([1, E, B])).then_inc(spread_done, 1)
                ve.wait_ge(mx_ready, 1)
                nc.vector.tensor_copy(mx[:, :], banks[1][:, 0:1]).then_inc(mx_done, 1)
                ve.wait_ge(mx_done, 1)
                nc.vector.tensor_scalar(dist[:, :], lgt[:, :], -1.0, mx[:, 0:1], ALU.mult, ALU.add)\
                    .then_inc(dist_done, 1)
                ve.wait_ge(z_ready, 1)
                nc.vector.tensor_copy(zcol[:, :], banks[2][:, 0:1]).then_inc(z_done, 1)
                ve.wait_ge(stats_ready, 1)
                nc.vector.tensor_scalar(nmxb[:, :], banks[3][:, 0:E], -1.0, None, ALU.mult)
                nc.vector.reciprocal(rzb[:, :], banks[3][:, E:2 * E]).then_inc(stats_done, 1)
                ve.wait_ge(dist_done, 1)

                def count_below(width):
                    for i in range(width):
                        m = nc.vector.tensor_scalar((below, ties, chosen)[i][:, :], dist[:, :],
                                                    cand[:, i:i + 1].bitcast(f32), None, ALU.is_lt,
                                                    ALU.add, accum_out=cnt[:, i:i + 1])
                    m.then_inc(cnt_done, 1)

                def raise_kth(r, width):
                    ve.wait_ge(total_ready, r + 1)
                    nc.vector.tensor_scalar(keep[:, 0:width], banks[0][:, 0:width], float(CAP), None, ALU.is_lt,
                                            ALU.add, accum_out=kept[:, :]).then_inc(keep_done, 1)
                    ve.wait_ge(keep_done, r + 1)
                    nc.vector.tensor_tensor(gain[:, :], kept[:, :], low[:, :], ALU.mult).then_inc(gain_done, 1)
                    ve.wait_ge(gain_done, r + 1)
                    nc.vector.tensor_tensor(kth[:, :], kth[:, :], gain[:, :], ALU.bitwise_or).then_inc(kth_done, 1)

                with ve.Fori(0, ROUNDS) as r:
                    ve.wait_ge(kth_done, r + 1)
                    ve.wait_ge(bit_done, r + 1)
                    nc.vector.tensor_tensor(cand[:, :], kth[:, :].to_broadcast([128, 3]), bits[:, :],
                                            ALU.bitwise_or).then_inc(cand_done, 1)
                    ve.wait_ge(cand_done, r + 1)
                    count_below(3)
                    nc.vector.tensor_scalar(bits[:, :], bits[:, :], 2, None, ALU.logical_shift_right)
                    raise_kth(r, 3)
                    nc.vector.tensor_scalar(low[:, :], low[:, :], 0.25, None, ALU.mult).then_inc(bit_done, 1)
                ve.wait_ge(kth_done, ROUNDS + 1)
                ve.wait_ge(bit_done, ROUNDS + 1)
                nc.vector.tensor_scalar(cand[:, 0:1], kth[:, :], 1, None, ALU.bitwise_or)
                nc.vector.memset(low[:, :], 1.0).then_inc(cand_done, 1)
                ve.wait_ge(cand_done, ROUNDS + 1)
                count_below(1)
                raise_kth(ROUNDS, 1)

                step = [0]

                def then(ins):
                    step[0] += 1
                    ins.then_inc(pick_step, 1)
                    ve.wait_ge(pick_step, step[0])

                ve.wait_ge(kth_done, ROUNDS + 2)
                edge = kth[:, :].bitcast(f32)
                then(nc.vector.tensor_scalar(below[:, :], dist[:, :], edge, None, ALU.is_lt, ALU.add,
                                             accum_out=nbelow[:, :]))
                then(nc.vector.tensor_scalar(ties[:, :], dist[:, :], edge, None, ALU.is_equal))
                then(nc.vector.tensor_tensor_scan(work[:, :], scan_one[:, :], ties[:, :], 0.0, ALU.mult, ALU.add))
                ve.wait_ge(ties_ready, 1)
                then(nc.vector.tensor_copy(col[:, 0:2], banks[1][:, 0:2]))
                then(nc.vector.tensor_tensor(col[:, 2:3], col[:, 0:1], col[:, 1:2], ALU.add))
                then(nc.vector.tensor_scalar(col[:, 2:3], col[:, 2:3], -1.0, float(CAP), ALU.mult, ALU.add))
                then(nc.vector.scalar_tensor_tensor(chosen[:, :], work[:, :], col[:, 2:3], ties[:, :],
                                                    ALU.is_le, ALU.mult))
                then(nc.vector.tensor_tensor(chosen[:, :], chosen[:, :], below[:, :], ALU.add))
                then(nc.vector.tensor_tensor_scan(slot[:, :], scan_one[:, :], chosen[:, :], 0.0, ALU.mult, ALU.add))
                ve.wait_ge(offset_ready, 1)
                then(nc.vector.tensor_copy(col[:, 0:1], banks[2][:, 0:1]))
                then(nc.vector.scalar_tensor_tensor(work[:, :], slot[:, :], col[:, 0:1], chosen[:, :],
                                                    ALU.add, ALU.mult))
                then(nc.vector.tensor_scalar(sloti[:, :], work[:, :], -1.0, None, ALU.add))
                then(nc.vector.tensor_scalar(hii[:, :], sloti[:, :], LO.bit_length() - 1, None,
                                             ALU.arith_shift_right))
                then(nc.vector.tensor_scalar(loi[:, :], sloti[:, :], LO - 1, None, ALU.bitwise_and))
                then(nc.vector.tensor_copy(hib[:, :], hii[:, :]))
                then(nc.vector.tensor_copy(lob[:, :], loi[:, :]))
                ve.wait_ge(split_ready, 1)
                for s, dst in enumerate((hiT, loT)):
                    for ch in range(CH):
                        src = banks[3 + 2 * s + ch // 4][0:T, :].bitcast(bf16)[:, (ch % 4) * 128:(ch % 4 + 1) * 128]
                        m = nc.vector.tensor_copy(
                            dst[:, :].rearrange("p (e c b) -> p e c b", e=E, c=CH)[:, :, ch, :],
                            src.rearrange("p (e b) -> p e b", e=E))
                m.then_inc(splitT_done, 1)

                def one_hots(k):
                    here = bass.ds(k * PX, PX) if not isinstance(k, int) else slice(k * PX, (k + 1) * PX)
                    ve.wait_ge(list_ready, k + 1)
                    for r in range(HI):
                        nc.vector.tensor_scalar(hot_hi[:, r, :], hiT[:, here], float(r), None, ALU.is_equal)
                    for r in range(LO):
                        m = nc.vector.tensor_scalar(hot_lo[:, r, :], loT[:, here], float(r), None, ALU.is_equal)
                    m.then_inc(hot_done, 1)
                    ve.wait_ge(hot_done, k + 1)
                    nc.vector.tensor_scalar(hot_lo[:, LO:2 * LO, :], hot_lo[:, 0:LO, :], c(ROW, T, 1), None,
                                            ALU.mult).then_inc(scaled_done, 1)
                    nc.vector.tensor_tensor(hot_lo[:, 2 * LO:3 * LO, :], hot_lo[:, 0:LO, :],
                                            tile_no[:, :].unsqueeze(1).to_broadcast([T, LO, PX]),
                                            ALU.mult).then_inc(scaled_done, 1)

                def tokens(k):
                    listed = ve.to_reg(ve.snap(k + 2)) if not isinstance(k, int) else k + 2
                    sent = ve.to_reg(ve.snap(32 * k + 32)) if not isinstance(k, int) else 32 * k + 32
                    ve.wait_ge(logits_in, 16)
                    ve.wait_ge(list_ready, listed)
                    nc.vector.tensor_copy(found[:, :, :, :].rearrange("p a b c -> p (a b c)"),
                                          banks[6][0:HI, 0:4 * LO]).then_inc(found_done, 1)
                    ve.wait_ge(found_done, k + 1)
                    ve.wait_ge(idx_in, sent)
                    nc.vector.scalar_tensor_tensor(ids[:, :, :], found[:, :, 1, :], float(T), found[:, :, 0, :],
                                                   ALU.mult, ALU.add).then_inc(ids_done, 1)

                def turn(k):
                    two = bass.ds(2 * k, 2) if not isinstance(k, int) else slice(2 * k, 2 * k + 2)
                    arrived = ve.to_reg(ve.snap(32 * k + 64)) if not isinstance(k, int) else 32 * k + 64
                    past = ve.to_reg(ve.snap(32 * ST * k)) if not isinstance(k, int) else 32 * ST * k
                    done = ve.to_reg(ve.snap(PER * k + 2)) if not isinstance(k, int) else PER * k + 2
                    ve.wait_ge(logits_in, 16)
                    ve.wait_ge(y_ready, done)
                    for i, src in enumerate((nmxb, rzb, wr_sb)):
                        m = nc.vector.tensor_scalar(cur[:, i, :], src[:, two], 1.0, None, ALU.mult)
                    m.then_inc(cur_done, 1)
                    for j in range(2):
                        for h in range(2):
                            ready = (ve.to_reg(ve.snap(PER * k + 2 * j + h + 2)) if not isinstance(k, int)
                                     else PER * k + 2 * j + h + 2)
                            ve.wait_ge(logits_in, 16)
                            ve.wait_ge(xsT_ready, ready)
                            nc.vector.tensor_copy(xsT[j][:, h * 512:(h + 1) * 512], banks[h][:, :])\
                                .then_inc(xsT_done, 1)
                    ve.wait_ge(logits_in, 16)
                    ve.wait_ge(idx_in, arrived)
                    if not isinstance(past, int) or past > 0:
                        ve.wait_ge(scattered, past)
                    nc.vector.tensor_copy(idx[:, :, :], idx_next[:, :, :]).then_inc(idx_done, 1)
                    ve.wait_ge(exp_done, k + 1)
                    nc.vector.tensor_tensor(val[:, :, :], val[:, :, :],
                                            cur[:, 1, :].unsqueeze(2).to_broadcast([128, 2, ST]), ALU.mult)\
                        .then_inc(val_done, 1)

                def expert(k, j):
                    for h in range(2):
                        ve.wait_ge(y_ready, (2 * k + j) * 2 + h + 3)
                        past = (2 * k + j) * 16 * ST
                        if not isinstance(past, int) or past > 0:
                            ve.wait_ge(scattered, past)
                        nc.vector.tensor_tensor(y[h][:, :, :], banks[4 + h][:, :].rearrange("p (g d) -> p g d", g=HALF_T),
                                                b2s[j][:, :].unsqueeze(1).to_broadcast([128, HALF_T, F]), ALU.add)\
                            .then_inc(y_done, 1)
                        ve.wait_ge(val_done, k + 2)
                        ve.wait_ge(y_done, (2 * k + j) * 2 + h + 3)
                        nc.vector.tensor_tensor(
                            y[h][:, :, :], y[h][:, :, :],
                            val[:, j, HALF_T * h:HALF_T * (h + 1)].unsqueeze(2).to_broadcast([128, HALF_T, F]),
                            ALU.mult).then_inc(yw_done, 1)

                ve.sem_inc(xsT_done, 2)
                ve.sem_inc(val_done, 1)
                ve.sem_inc(y_done, 2)
                ve.sem_inc(yw_done, 1)
                ve.wait_ge(splitT_done, 1)
                one_hots(0)
                tokens(0)
                one_hots(1)
                tokens(1)

                def pair(k):
                    turn(k)
                    one_hots(k + 2)
                    expert(k, 0)
                    tokens(k + 2)
                    expert(k, 1)

                pair(0)
                with ve.Fori(1, PAIRS - 2) as k:
                    pair(k)
                with ve.Fori(PAIRS - 2, PAIRS) as k:
                    turn(k)
                    expert(k, 0)
                    expert(k, 1)

            @block.gpsimd
            def _(po):
                rows = out.rearrange("b t f -> (b t) f")

                def reg(k, value):
                    return value if isinstance(k, int) else po.to_reg(po.snap(value))

                def gather(k):
                    for j in range(2):
                        listed, turned = reg(k, 32 * k + 64), reg(k, PER * k + 1)
                        po.wait_ge(logits_in, 16)
                        po.wait_ge(idx_in, listed)
                        po.wait_ge(xsT_ready, turned)
                        for g in range(ST):
                            nc.gpsimd.indirect_dma_start(
                                xs[j][:, g, :], None, x2_rows,
                                bass.IndirectOffsetOnAxis(idx_next[:, j, g:g + 1], 0)).then_inc(gathered[j], 16)

                def expert(k, j):
                    for h in range(2):
                        weighted = reg(k, (2 * k + j) * 2 + h + 2)
                        added = reg(k, (2 * k + j) * 16 * ST)
                        po.wait_ge(logits_in, 16)
                        po.wait_ge(yw_done, weighted)
                        if h == 0 and (not isinstance(added, int) or added > 0):
                            po.wait_ge(scattered, added)
                        for g in range(HALF_T):
                            nc.gpsimd.indirect_dma_start(
                                rows, bass.IndirectOffsetOnAxis(idx[:, j, HALF_T * h + g:HALF_T * h + g + 1], 0),
                                y[h][:, g, :], None, compute_op=ALU.add).then_inc(scattered, 16)

                po.sem_inc(idx_in, 32)
                po.sem_inc(xsT_ready, 1)
                gather(0)

                def pair(k):
                    gather(k + 1)
                    expert(k, 0)
                    expert(k, 1)

                pair(0)
                with po.Fori(1, PAIRS - 1) as k:
                    pair(k)
                expert(PAIRS - 1, 0)
                expert(PAIRS - 1, 1)
                po.wait_ge(scattered, 16 * ST * E)


def kernel(**inputs):
    import concourse.bacc as _bacc
    from concourse import mybir as _mybir
    from concourse.bass_utils import run_bass_kernel_spmd as _run

    a = {k: np.asarray(v) for k, v in inputs.items()}

    def col(name):
        return a[name].reshape(-1, 128).T

    vecs = np.concatenate(
        [col("L0_tok_bias")] + [col("L0_attn_b" + s) for s in "qkvg"]
        + [a["L0_attn_cw" + s][:, 0, :] for s in "qkv"] + [col("L0_attn_cb" + s) for s in "qkv"]
        + [col("L0_attn_norm_w"), col("L0_attn_bo")], axis=1)
    arrays = {
        "in_x": a["x"], "in_consts": constants(), "in_vecs": vecs,
        "in_wconv": a["L0_tok_kernel"].reshape(TAPS * CIN, F),
        "in_wlin": np.stack([a["L0_attn_W" + s].T for s in "qkvgo"]),
        "in_wab": np.concatenate([a["L0_attn_Wa"].T, a["L0_attn_Wb"].T], axis=1),
        "in_bab": np.concatenate([a["L0_attn_ba"], a["L0_attn_bb"]]),
        "in_wr": a["L0_ffn_Wr"], "in_w1": a["L0_ffn_W1"],
        "in_b1": a["L0_ffn_b1"].reshape(E, FF // 128, 128).transpose(2, 0, 1),
        "in_w2": a["L0_ffn_W2"], "in_b2": a["L0_ffn_b2"].reshape(E * 128),
    }
    arrays = {k: np.ascontiguousarray(v) for k, v in arrays.items()}
    nc = _bacc.Bacc("TRN2", target_bir_lowering=False, num_devices=1)
    args = [nc.dram_tensor(k, v.shape, _mybir.dt.from_np(v.dtype), kind="ExternalInput").ap()
            for k, v in arrays.items()]
    out = nc.dram_tensor("out_0", (B, L, F), _mybir.dt.float32, kind="ExternalOutput").ap()
    x2_rows = nc.dram_tensor("x2_rows", (N, F), _mybir.dt.float32, kind="Internal").ap()
    logits = nc.dram_tensor("logits", (E, B, L), _mybir.dt.float32, kind="Internal").ap()
    tower(nc, *args, out, x2_rows, logits)
    r = _run(nc, [arrays], core_ids=[0])
    return r.results[0]["out_0"]
```
